# Optimizing a Trainium2 kernel written in Bass

```python
import numpy as np
import jax
import jax.numpy as jnp

def _softmax(x, axis=-1):
    return jax.nn.softmax(x, axis=axis)

def _gelu(x):
    return jax.nn.gelu(x, approximate=True)

def _silu(x):
    return jax.nn.silu(x)

def _sigmoid(x):
    return jax.nn.sigmoid(x)

def _layernorm(x, axis=-1, eps=1e-05):
    m = jnp.mean(x, axis=axis, keepdims=True)
    v = jnp.var(x, axis=axis, keepdims=True)
    return (x - m) / jnp.sqrt(v + eps)

def _scatter_add(tgt, idx, src, axis=0):
    return tgt.at[idx].add(src)

def _segment_sum(src, seg, n):
    return jax.ops.segment_sum(src, seg, n)
kernel_name = 'mk_xattn_ffn_d1_seqx_r8_330262'

def setup_inputs(seed: int=0):
    np.random.seed(seed)
    _w = jnp.asarray

    def _rec_inputs():
        import jax
        import jax.numpy as jnp
        _rk = jax.random.key(seed)
        x = -0.0002928 + 1 * jax.random.normal(jax.random.fold_in(_rk, 1), (16, 100, 128), jnp.float32)
        _lenS = 100 - jax.random.randint(jax.random.fold_in(_rk, 7), (16,), 0, max(1, 100 // 4) + 1, jnp.int32)
        _lenS2 = 1444 - jax.random.randint(jax.random.fold_in(_rk, 8), (16,), 0, max(1, 1444 // 4) + 1, jnp.int32)
        _ctx_1024P = jax.random.normal(jax.random.fold_in(_rk, 11), (16, 16, 128), jnp.float32)
        _ctx_1024c = jax.random.dirichlet(jax.random.fold_in(_rk, 511), 0.3 * jnp.ones((16,), jnp.float32), (16, 1444))
        _ctx_1024t = jnp.einsum('bsk,bkd->bsd', _ctx_1024c, _ctx_1024P)
        _ctx_1024t = _ctx_1024t * jax.lax.rsqrt(jnp.mean(jnp.square(_ctx_1024t)) + 1e-12) * 0.953939
        ctx_1024 = -1.39393e-06 + 0.999914 * (_ctx_1024t + 0.3 * jax.random.normal(jax.random.fold_in(_rk, 611), (16, 1444, 128), jnp.float32))
        _validS = jnp.arange(100)[None, :] < _lenS[:, None]
        _validS2 = jnp.arange(1444)[None, :] < _lenS2[:, None]
        _causal = jnp.tril(jnp.ones((100, 100), dtype=bool))
        mask_Bx1xSxS2_bf0 = jnp.logical_not(jnp.ones((16, 1, 100, 1444), dtype=bool))
        return (x, ctx_1024, mask_Bx1xSxS2_bf0)
    x, ctx_1024, mask_Bx1xSxS2_bf0 = _rec_inputs()

    def _L0_xattn_setup():
        import jax, jax.numpy as jnp
        import numpy as np
        B, S, D, H = (2, 256, 128, 16)
        HD = D // H
        LN_EPS = 1e-05

        def _linear(x, w, b):
            return jnp.einsum('bsd,od->bso', x, w) + b

        def _split_heads(x):
            b, s, _ = x.shape
            return x.reshape(b, s, H, HD).transpose(0, 2, 1, 3)
        key = jax.random.key(seed)
        ks = jax.random.split(key, 14)
        w = 0.02
        return {'q': jax.random.normal(ks[0], (B, S, D), jnp.float32), 'k': jax.random.normal(ks[1], (B, S, D), jnp.float32), 'v': jax.random.normal(ks[2], (B, S, D), jnp.float32), 'mask': jnp.zeros((B, 1, S, S), dtype=bool), 'training': 0, 'wq_w': jax.random.normal(ks[3], (D, D), jnp.float32) * w, 'wq_b': jnp.zeros((D,), jnp.float32), 'wk_w': jax.random.normal(ks[4], (D, D), jnp.float32) * w, 'wk_b': jnp.zeros((D,), jnp.float32), 'wv_w': jax.random.normal(ks[5], (D, D), jnp.float32) * w, 'wv_b': jnp.zeros((D,), jnp.float32), 'wo_w': jax.random.normal(ks[6], (D, D), jnp.float32) * w, 'wo_b': jnp.zeros((D,), jnp.float32), 'ln_g': jnp.ones((D,), jnp.float32), 'ln_b': jnp.zeros((D,), jnp.float32)}
    _L0_xattn_all = _L0_xattn_setup()
    _L0_xattn_in = {k: v for k, v in _L0_xattn_all.items() if k in ('wq_w', 'wq_b', 'wk_w', 'wk_b', 'wv_w', 'wv_b', 'wo_w', 'wo_b', 'ln_g', 'ln_b')}
    del _L0_xattn_all

    def _L0_ffn_setup():
        import jax, jax.numpy as jnp
        import numpy as np
        B, S, DIM, FFN, E = (4, 256, 128, 512, 8)
        key = jax.random.key(seed)
        k0, k1, k2, k3 = jax.random.split(key, 4)
        scale = 0.02
        return {'hidden_states': jax.random.normal(k0, (B, S, DIM), jnp.float32), 'router_w': jax.random.normal(k1, (DIM, E), jnp.float32) * scale, 'router_b': jnp.zeros((E,), jnp.float32), 'w1': jax.random.normal(k2, (E, DIM, 2 * FFN), jnp.float32) * scale, 'w2': jax.random.normal(k3, (E, FFN, DIM), jnp.float32) * scale}
    _L0_ffn_all = _L0_ffn_setup()
    _L0_ffn_in = {k: v for k, v in _L0_ffn_all.items() if k in ('router_w', 'router_b', 'w1', 'w2')}
    del _L0_ffn_all
    return {'x': x, 'ctx_1024': ctx_1024, 'mask_Bx1xSxS2_bf0': mask_Bx1xSxS2_bf0, 'L0_xattn_wq_w': _L0_xattn_in['wq_w'], 'L0_xattn_wq_b': _L0_xattn_in['wq_b'], 'L0_xattn_wk_w': _L0_xattn_in['wk_w'], 'L0_xattn_wk_b': _L0_xattn_in['wk_b'], 'L0_xattn_wv_w': _L0_xattn_in['wv_w'], 'L0_xattn_wv_b': _L0_xattn_in['wv_b'], 'L0_xattn_wo_w': _L0_xattn_in['wo_w'], 'L0_xattn_wo_b': _L0_xattn_in['wo_b'], 'L0_xattn_ln_g': _L0_xattn_in['ln_g'], 'L0_xattn_ln_b': _L0_xattn_in['ln_b'], 'L0_ffn_router_w': _L0_ffn_in['router_w'], 'L0_ffn_router_b': _L0_ffn_in['router_b'], 'L0_ffn_w1': _L0_ffn_in['w1'], 'L0_ffn_w2': _L0_ffn_in['w2']}

def reference(x, ctx_1024, mask_Bx1xSxS2_bf0, L0_xattn_wq_w, L0_xattn_wq_b, L0_xattn_wk_w, L0_xattn_wk_b, L0_xattn_wv_w, L0_xattn_wv_b, L0_xattn_wo_w, L0_xattn_wo_b, L0_xattn_ln_g, L0_xattn_ln_b, L0_ffn_router_w, L0_ffn_router_b, L0_ffn_w1, L0_ffn_w2):
    import jax
    import jax.numpy as jnp

    def _L0_xattn_ref(q, k, v, mask, training, wq_w, wq_b, wk_w, wk_b, wv_w, wv_b, wo_w, wo_b, ln_g, ln_b):
        import jax, jax.numpy as jnp
        import numpy as np
        B, S, D, H = (2, 256, 128, 16)
        HD = D // H
        LN_EPS = 1e-05

        def _linear(x, w, b):
            return jnp.einsum('bsd,od->bso', x, w) + b

        def _split_heads(x):
            b, s, _ = x.shape
            return x.reshape(b, s, H, HD).transpose(0, 2, 1, 3)
        residual = q
        Q = _split_heads(_linear(q, wq_w, wq_b))
        K = _split_heads(_linear(k, wk_w, wk_b))
        V = _split_heads(_linear(v, wv_w, wv_b))
        dk = jnp.sqrt(jnp.asarray(HD, jnp.float16)).astype(jnp.float32) + 1e-08
        score = jnp.einsum('bhqd,bhkd->bhqk', Q, K) / dk
        attn = jnp.where(mask, -jnp.inf, score)
        ctx = jnp.einsum('bhqk,bhkd->bhqd', attn, V)
        b, _, s, _ = ctx.shape
        ctx = ctx.transpose(0, 2, 1, 3).reshape(b, s, D)
        o = _linear(ctx, wo_w, wo_b)
        x = residual + o
        mu = jnp.mean(x, axis=-1, keepdims=True)
        var = jnp.mean(jnp.square(x - mu), axis=-1, keepdims=True)
        return ln_g * (x - mu) * jax.lax.rsqrt(var + LN_EPS) + ln_b

    def _L0_ffn_ref(hidden_states, router_w, router_b, w1, w2):
        import jax, jax.numpy as jnp
        import numpy as np
        B, S, DIM, FFN, E = (4, 256, 128, 512, 8)
        b, s, d = hidden_states.shape
        x = hidden_states.reshape(-1, d)
        logits = x @ router_w + router_b
        route = jax.nn.softmax(logits, axis=1)
        max_prob = jnp.max(route, axis=1, keepdims=True)
        max_ind = jnp.argmax(route, axis=1)
        out = jnp.zeros_like(x)
        num_experts = w1.shape[0]
        for e in range(num_experts):
            h = x @ w1[e]
            a, g = jnp.split(h, 2, axis=1)
            y = jax.nn.silu(a) * g @ w2[e]
            out = jnp.where((max_ind == e)[:, None], y, out)
        out = out * max_prob
        return out.reshape(b, s, d)
    x = x + _L0_xattn_ref(_layernorm(x, axis=-1), ctx_1024, ctx_1024, mask_Bx1xSxS2_bf0, 0, L0_xattn_wq_w, L0_xattn_wq_b, L0_xattn_wk_w, L0_xattn_wk_b, L0_xattn_wv_w, L0_xattn_wv_b, L0_xattn_wo_w, L0_xattn_wo_b, L0_xattn_ln_g, L0_xattn_ln_b)
    x = x + _L0_ffn_ref(_layernorm(x, axis=-1), L0_ffn_router_w, L0_ffn_router_b, L0_ffn_w1, L0_ffn_w2)
    return x

_drawn_inputs = setup_inputs


def setup_inputs(seed=0):
    import zlib

    import numpy as np

    out = dict(_drawn_inputs(seed))
    spreads = {'L0_xattn_wq_b': (0.0, 0.1),
     'L0_xattn_wk_b': (0.0, 0.1),
     'L0_xattn_wv_b': (0.0, 0.1),
     'L0_xattn_wo_b': (0.0, 0.298),
     'L0_xattn_ln_g': (1.0, 0.2),
     'L0_xattn_ln_b': (0.0, 0.1),
     'L0_ffn_router_b': (0.0, 0.8)}
    factors = {'L0_ffn_router_w': 8.0, 'L0_ffn_w1': 8.0, 'L0_ffn_w2': 8.0}
    for name, (base, spread) in spreads.items():
        noise = np.random.default_rng([zlib.crc32(name.encode()), seed]).standard_normal(out[name].shape)
        drawn = base * np.exp(spread * noise) if base else spread * noise
        out[name] = jnp.asarray(drawn.astype(out[name].dtype))
    for name, factor in factors.items():
        out[name] = (out[name] * factor).astype(out[name].dtype)
    return out
```

```python
from contextlib import ExitStack

import concourse.bass as bass
from concourse import mybir

ALU = mybir.AluOpType
ACT = mybir.ActivationFunctionType
AX = mybir.AxisListType.X
F32 = mybir.dt.float32
BF16 = mybir.dt.bfloat16
I32 = mybir.dt.int32
U8 = mybir.dt.uint8

P = 128
LN_EPS = 1e-5
HEADS = 16
DK = 2.828125
GUESS = 1597463007.0
NEWTON_STEPS = 3
NAN_BITS = 2143289344.0
SKIP = 1000000


class Steps:

    def __init__(self, engine, semaphore):
        self.engine, self.semaphore, self.base, self.count = engine, semaphore, 0, 0

    def begin(self, base):
        self.base, self.count = base, 0

    def done(self, instruction):
        instruction.then_inc(self.semaphore, 1)
        self.count += 1

    def then(self):
        self.engine.wait_ge(self.semaphore, self.base + self.count)


def build(nc, x, ctx_rows, mask, wq_w, wq_b, wk_w, wk_b, wv_w, wv_b, wo_w, wo_b, ln_g, ln_b,
          router_w, router_b, w1, w2, out):
    B, S, D = x.shape
    S2 = ctx_rows.shape[1]
    E, _, F2 = w1.shape
    FF = F2 // 2
    HD = D // HEADS
    assert D == P and HD == 8 and FF % P == 0

    GB = 4
    NG = B // GB
    FULL = S2 // P
    REST = S2 - FULL * P
    NCH = FULL + 1
    CW = D + 1
    TOKENS = B * S
    TILES = (TOKENS + E * (P - 1)) // P
    ROW = D + 3
    MEAN, RSTD, GATE = D, D + 1, D + 2
    FC = FF // P
    MW = S2 // 4
    NT_MAX = (TOKENS + P - 1) // P
    COLS = E * NT_MAX

    token_rows = nc.dram_tensor("token_rows", (TOKENS, ROW), F32, kind="Internal").ap()
    slot_map = nc.dram_tensor("slot_map", (P * COLS, 1), I32, kind="Internal").ap()
    out_rows = out.rearrange("b s d -> (b s) d")

    with ExitStack() as stack:
        def sb(name, shape, dtype=F32):
            return stack.enter_context(nc.sbuf_tensor(name, shape, dtype))

        def bank(name, shape):
            return stack.enter_context(nc.psum_tensor(name, shape, F32))

        def sem(name):
            return stack.enter_context(nc.semaphore(name))

        x_all = sb("x_all", [S, B * D])
        w_raw = sb("w_raw", [P, 4, D])
        w_T = sb("w_T", [P, 4, D])
        bk_rows = sb("bk_rows", [P, D])
        bv_rows = sb("bv_rows", [P, D])
        bo_rows = sb("bo_rows", [S, D])
        g_rows = sb("g_rows", [S, D])
        b_rows = sb("b_rows", [S, D])
        rb_rows = sb("rb_rows", [S, E])
        rw = sb("rw", [P, E])
        b_cols = sb("b_cols", [P, 2])
        bq_dk = sb("bq_dk", [P, 1])
        bk_s2 = sb("bk_s2", [P, 1])
        w1_sb = sb("w1_sb", [P, E * F2])
        w2_sb = sb("w2_sb", [P, E * FC * D])
        ident = sb("ident", [P, P])
        head_mask = sb("head_mask", [P, D])
        bv_mask = sb("bv_mask", [P, D])
        before = sb("before", [S, S], BF16)
        ones = sb("ones", [S, P], BF16)
        first_w = sb("first_w", [S, GB, E])

        ctx_sb = sb("ctx_sb", [P, GB, NCH, CW])
        gram = sb("gram", [P, GB, CW])
        s_bk = sb("s_bk", [P, GB, D])
        w4 = sb("w4", [P, GB])
        w_bv = sb("w_bv", [P, GB, D])
        u_sb = sb("u_sb", [P, GB, D])
        m_own = sb("m_own", [P, GB, D])
        m_sb = sb("m_sb", [P, GB, D])
        xln = sb("xln", [S, GB, D])
        xlnT = sb("xlnT", [P, GB * S])
        qT = sb("qT", [P, GB * S])
        ctxT = sb("ctxT", [P, GB * S])
        q_bo = sb("q_bo", [S, GB, D])
        x_b = sb("x_b", [S, GB, D])
        res = sb("res", [S, GB, D])
        nrm = sb("nrm", [S, GB, D])
        rows = sb("rows", [S, GB, ROW])
        h_sb = sb("h_sb", [S, GB, D])
        hT = sb("hT", [P, GB * S])
        stats = sb("stats", [S, B, 6])
        mv = sb("mv", [S, B, 2])
        ve = sb("ve", [S, B])
        half = sb("half", [S, B])
        y0 = sb("y0", [S, B])
        sq = sb("sq", [S, B])
        x_rstd = sb("x_rstd", [S, B])
        x_nb = sb("x_nb", [S, B])
        mask_sb = sb("mask_sb", [S, GB, S2], U8)
        masked = sb("masked", [S, GB])
        nan_or_0 = sb("nan_or_0", [S, GB], I32)

        logit = sb("logit", [S, GB, E])
        below = sb("below", [S, GB, E])
        best = sb("best", [S, GB])
        score = sb("score", [S, GB, E])
        choice = sb("choice", [S, GB, E], BF16)
        th = sb("th", [S, GB, E])
        e1 = sb("e1", [S, GB, E])
        e2 = sb("e2", [S, GB, E])
        e3 = sb("e3", [S, GB, E])
        esum = sb("esum", [S, GB])
        rank = sb("rank", [S, GB, E])
        pos = sb("pos", [S, GB])
        pos_i = sb("pos_i", [S, GB], I32)
        low = sb("low", [S, GB], I32)
        high = sb("high", [S, GB], I32)
        map_i = sb("map_i", [S, GB], I32)
        next_i = sb("next_i", [P, E], I32)
        region = sb("region", [P, E])
        next_free = sb("next_free", [P, E])
        row_no = sb("row_no", [S, GB], I32)

        count = sb("count", [P, E])
        stair_i = sb("stair_i", [P, NT_MAX], I32)
        stair = sb("stair", [P, NT_MAX])
        tile_i = sb("tile_i", [P, TILES], I32)
        tile_no = sb("tile_no", [P, TILES])
        e_i = sb("e_i", [P, E], I32)
        e_no = sb("e_no", [P, E])
        upto = sb("upto", [P, E, E])
        more = sb("more", [P, E, NT_MAX])
        nt = sb("nt", [P, E])
        nt_all = sb("nt_all", [P, E, E])
        end = sb("end", [P, E])
        first = sb("first", [P, E])
        own_a = sb("own_a", [P, TILES, E])
        own_b = sb("own_b", [P, TILES, E])
        own = sb("own", [P, TILES, E])
        pick = sb("pick", [P, 2, TILES, E])
        from_e = sb("from_e", [P, E])
        col_te = sb("col_te", [P, TILES, E])
        picked = sb("picked", [P, 2, TILES])
        col_i = sb("col_i", [P, TILES], I32)
        expert_i = sb("expert_i", [P, TILES], I32)

        map_sb = sb("map_sb", [P, COLS + 1], I32)
        token = sb("token", [P, TILES], I32)
        slots = sb("slots", [P, TILES * ROW])
        h2 = sb("h2", [P, 2, D])
        h2T = sb("h2T", [P, 2, P])
        gate_s = sb("gate_s", [P, 2, FF])
        act = sb("act", [P, 2, FF])
        actT = sb("actT", [P, 2, FF])
        out_sb = sb("out_sb", [P, 2, D])

        bank_g = [bank("bank_g0", [P, 512]), bank("bank_g1", [P, 512])]
        bank_c, bank_u, bank_m = bank("bank_c", [P, 512]), bank("bank_u", [P, 512]), bank("bank_m", [P, 512])
        bank_x, bank_q, bank_r = bank("bank_x", [P, 512]), bank("bank_q", [P, 512]), bank("bank_r", [P, 512])
        ps_w = bank_r[:, 0:GB]
        ps_logit = bank_r[0:S, 64:64 + GB * E]
        ps_rank = bank_r[0:S, 128:128 + GB * E]
        ps_count = bank_r[:, 192:192 + E]

        x_in, w_in, small_in, w1_in, w2_in = sem("x_in"), sem("w_in"), sem("small_in"), sem("w1_in"), sem("w2_in")
        ctx_in = [sem(f"ctx_in{j}") for j in range(GB)]
        mask_in = sem("mask_in")
        ones_set = sem("ones_set")
        pool_set = sem("pool_set")
        ident_set = sem("ident_set")
        wT_done, wT_kept = sem("wT_done"), sem("wT_kept")
        consts_ready = sem("consts_ready")
        x_stats = sem("x_stats")
        gram_done = sem("gram_done")
        gram_kept = sem("gram_kept")
        xln_ready = sem("xln_ready")
        xlnT_done, xlnT_kept = sem("xlnT_done"), sem("xlnT_kept")
        q_done, q_kept = sem("q_done"), sem("q_kept")
        q_bo_ready, x_b_ready = sem("q_bo_ready"), sem("x_b_ready")
        s_bk_ready = sem("s_bk_ready")
        u_done, u_kept = sem("u_done"), sem("u_kept")
        w_done, w4_ready, w_bv_ready = sem("w_done"), sem("w4_ready"), sem("w_bv_ready")
        m_done, m_kept = sem("m_done"), sem("m_kept")
        c_done, c_kept = sem("c_done"), sem("c_kept")
        o_done, res_ready = sem("o_done"), sem("res_ready")
        x1_ready, h_ready = sem("x1_ready"), sem("h_ready")
        hT_done, hT_kept = sem("hT_done"), sem("hT_kept")
        logit_done, below_ready, th_ready = sem("logit_done"), sem("below_ready"), sem("th_ready")
        choice_ready, rank_done, rank_kept = sem("choice_ready"), sem("rank_done"), sem("rank_kept")
        rows_ready = sem("rows_ready")
        mask_used = sem("mask_used")
        map_set = sem("map_set")
        rows_out = sem("rows_out")
        map_out = sem("map_out")
        map_in = sem("map_in")
        token_ready = sem("token_ready")
        dve = sem("dve_step")
        table_ready = sem("table_ready")
        gathered = [sem("gathered0"), sem("gathered1")]
        h2_ready, h2T_done, h2T_kept = sem("h2_ready"), sem("h2T_done"), sem("h2T_kept")
        a_done, silu_done, g_done, act_ready = sem("a_done"), sem("silu_done"), sem("g_done"), sem("act_ready")
        actT_done, actT_kept = sem("actT_done"), sem("actT_kept")
        y_done, out_ready = sem("y_done"), sem("out_ready")
        out_written = [sem("out_written0"), sem("out_written1")]

        block = stack.enter_context(nc.Block())

        def is_first(g):
            return isinstance(g, int) and g == 0

        def wait_alone(engine, semaphore, value, sure, sure_value):
            value = value if isinstance(value, int) else engine.snap(value)
            engine.wait_ge(sure, sure_value)
            engine.wait_ge(semaphore, value)

        def load_group(sp, g):
            for j in range(GB):
                b = g * GB + j
                row = ctx_rows[bass.ds(b, 1)].rearrange("o s d -> (o s) d")
                if is_first(g):
                    sp.wait_ge(ones_set, 1)
                else:
                    wait_alone(sp, gram_done, GB * (g - 1) + j + 1, ones_set, 1)
                sp.dma_start(ctx_sb[:, j, 0:FULL, 0:D],
                             row[0:FULL * P, :].rearrange("(p c) d -> p c d", p=P)).then_inc(ctx_in[j], 16)
                sp.dma_start(ctx_sb[0:REST, j, FULL, 0:D], row[FULL * P:S2, :]).then_inc(ctx_in[j], 16)
            if not is_first(g):
                wait_alone(sp, mask_used, g, ones_set, 1)
            sp.dma_start(mask_sb[:, :, :], mask[bass.ds(g * GB, GB), 0].rearrange("b q k -> q b k")).then_inc(mask_in, 16)

        @block.sync
        def _(sp):
            sp.dma_start(x_all[:, :].rearrange("q (b d) -> q b d", b=B), x.rearrange("b q d -> q b d")).then_inc(x_in, 16)
            load_group(sp, 0)
            with sp.Fori(1, NG) as g:
                load_group(sp, g)
            for e in range(E):
                sp.dma_start(w1_sb[:, e * F2:(e + 1) * F2], w1[e]).then_inc(w1_in, 16)
                sp.dma_start(w2_sb[:, e * FC * D:(e + 1) * FC * D].rearrange("p (c d) -> p c d", c=FC),
                             w2[e].rearrange("(c p) d -> p c d", p=P)).then_inc(w2_in, 16)

        @block.gpsimd
        def _(pool):
            pool.memset(ctx_sb[:, :, FULL, :], 0.0).then_inc(pool_set, 1)
            pool.memset(ident[:, :], 0.0).then_inc(pool_set, 1)
            pool.wait_ge(pool_set, 2)
            pool.memset(ctx_sb[:, :, :, D:CW], 1.0).then_inc(ones_set, 1)
            pool.affine_select(out=ident[:, :], in_=ident[:, :], compare_op=ALU.not_equal, fill=1.0,
                               base=0, pattern=[[-1, P]], channel_multiplier=1).then_inc(ident_set, 1)
            pool.memset(head_mask[:, :], 1.0).then_inc(pool_set, 1)
            pool.memset(before[:, :], 1.0).then_inc(pool_set, 1)
            pool.memset(ones[:, :], 1.0).then_inc(pool_set, 1)
            pool.memset(upto[:, :, :], 1.0).then_inc(pool_set, 1)
            pool.wait_ge(pool_set, 6)
            heads = head_mask[:, :].rearrange("p (h d) -> p h d", d=HD)
            pool.affine_select(out=heads, in_=heads, compare_op=ALU.is_ge, fill=0.0, base=0,
                               pattern=[[-HD, HEADS], [0, HD]], channel_multiplier=1).then_inc(pool_set, 1)
            pool.affine_select(out=before[:, :], in_=before[:, :], compare_op=ALU.is_gt, fill=0.0, base=0,
                               pattern=[[1, S]], channel_multiplier=-1).then_inc(pool_set, 1)
            pool.affine_select(out=upto[:, :, :], in_=upto[:, :, :], compare_op=ALU.is_ge, fill=0.0, base=0,
                               pattern=[[1, E], [-1, E]], channel_multiplier=0).then_inc(pool_set, 1)
            pool.wait_ge(pool_set, 9)
            pool.affine_select(out=heads, in_=heads, compare_op=ALU.is_ge, fill=0.0, base=HD - 1,
                               pattern=[[HD, HEADS], [0, HD]], channel_multiplier=-1).then_inc(pool_set, 1)
            pool.iota(row_no[:, :], pattern=[[S, GB]], base=-GB * S, channel_multiplier=1).then_inc(pool_set, 1)
            pool.iota(next_i[:, :], pattern=[[NT_MAX * P, E]], base=0, channel_multiplier=0).then_inc(pool_set, 1)
            pool.iota(stair_i[:, :], pattern=[[P, NT_MAX]], base=0, channel_multiplier=0).then_inc(pool_set, 1)
            pool.memset(map_sb[:, :], SKIP).then_inc(pool_set, 1)
            pool.iota(tile_i[:, :], pattern=[[1, TILES]], base=0, channel_multiplier=0).then_inc(pool_set, 1)
            pool.iota(e_i[:, :], pattern=[[1, E]], base=0, channel_multiplier=0).then_inc(pool_set, 1)
            pool.memset(slots[:, :], 0.0).then_inc(pool_set, 1)
            pool.wait_ge(pool_set, 17)
            map_2d = slot_map.rearrange("(p c) o -> p (c o)", p=P)
            pool.dma_start(map_2d, map_sb[:, 0:COLS]).then_inc(map_set, 16)
            last_slot = pool.to_reg(P * COLS - 1)
            last_token = pool.to_reg(TOKENS - 1)

            def prepare(g):
                pool.wait_ge(xln_ready, g + 1)
                if not is_first(g):
                    pool.wait_ge(x1_ready, g)
                else:
                    pool.wait_ge(small_in, 16 * 9)
                pool.tensor_tensor(q_bo[:, :, :], xln[:, :, :],
                                   bo_rows[:, :].unsqueeze(1).to_broadcast([S, GB, D]), ALU.add).then_inc(q_bo_ready, 1)
                pool.tensor_tensor(x_b[:, :, :],
                                   x_all[:, bass.ds(g * (GB * D), GB * D)].rearrange("q (b d) -> q b d", b=GB),
                                   b_rows[:, :].unsqueeze(1).to_broadcast([S, GB, D]), ALU.add).then_inc(x_b_ready, 1)

            def outer(h):
                if not is_first(h):
                    pool.wait_ge(m_kept, h)
                else:
                    pool.wait_ge(consts_ready, 1)
                pool.wait_ge(w4_ready, h + 1)
                pool.tensor_tensor(w_bv[:, :, :], bv_mask[:, :].unsqueeze(1).to_broadcast([P, GB, D]),
                                   w4[:, :].unsqueeze(2).to_broadcast([P, GB, D]), ALU.mult).then_inc(w_bv_ready, 1)

            def route(h):
                if is_first(h):
                    pool.wait_ge(map_set, 16)
                wait_alone(pool, rows_ready, h + 1, consts_ready, 1)
                for j in range(GB):
                    pool.indirect_dma_start(out=slot_map[:, :], out_offset=bass.IndirectOffsetOnAxis(ap=map_i[:, j:j + 1], axis=0),
                                            in_=row_no[:, j:j + 1], in_offset=None, bounds_check=last_slot,
                                            oob_is_err=False).then_inc(map_out, 16)
                pool.dma_start(token_rows[bass.ds(h * (GB * S), GB * S), :].rearrange("(j q) n -> q j n", j=GB),
                               rows[:, :, :]).then_inc(rows_out, 16)

            def round_of(g):
                outer(g - 1)
                prepare(g)
                route(g - 1)

            prepare(0)
            round_of(1)
            with pool.Fori(2, NG) as g:
                round_of(g)
            outer(NG - 1)
            route(NG - 1)

            AHEAD = 5

            def gather(t):
                column = pool.value_load(col_i[0:1, t:t + 1], min_val=0, max_val=COLS)
                pool.tensor_copy(token[:, t:t + 1], map_sb[:, bass.ds(column, 1)]).then_inc(token_ready, 1)
                if t >= 2:
                    pool.wait_ge(gathered[t % 2], 16 * (t // 2))
                pool.wait_ge(token_ready, t + 1)
                pool.indirect_dma_start(out=slots[:, t * ROW:(t + 1) * ROW], out_offset=None, in_=token_rows[:, :],
                                        in_offset=bass.IndirectOffsetOnAxis(ap=token[:, t:t + 1], axis=0),
                                        bounds_check=last_token, oob_is_err=False).then_inc(gathered[t % 2], 16)

            pool.wait_ge(map_out, 16 * GB * NG)
            pool.dma_start(map_sb[:, 0:COLS], map_2d).then_inc(map_in, 16)
            pool.wait_ge(rows_out, 16 * NG)
            pool.wait_ge(map_in, 16)
            pool.wait_ge(table_ready, 1)
            for t in range(AHEAD):
                gather(t)
            for t in range(TILES):
                if t + AHEAD < TILES:
                    gather(t + AHEAD)
                pool.wait_ge(out_ready, t + 1)
                pool.indirect_dma_start(out=out_rows[:, :], out_offset=bass.IndirectOffsetOnAxis(ap=token[:, t:t + 1], axis=0),
                                        in_=out_sb[:, t % 2, :], in_offset=None, bounds_check=last_token,
                                        oob_is_err=False).then_inc(out_written[t % 2], 16)
            pool.wait_ge(out_written[0], 16 * ((TILES + 1) // 2))
            pool.wait_ge(out_written[1], 16 * (TILES // 2))

        @block.scalar
        def _(act_):
            for n, w in enumerate((wq_w, wk_w, wv_w, wo_w)):
                act_.dma_start(w_raw[:, n, :], w[:, :]).then_inc(w_in, 16)
            for rows_of, src, n in ((bk_rows, wk_b, P), (bv_rows, wv_b, P), (bo_rows, wo_b, S), (g_rows, ln_g, S), (b_rows, ln_b, S)):
                act_.dma_start(rows_of[:, :], src.rearrange("(o d) -> o d", o=1).to_broadcast([n, D])).then_inc(small_in, 16)
            act_.dma_start(rb_rows[:, :], router_b.rearrange("(o d) -> o d", o=1).to_broadcast([S, E])).then_inc(small_in, 16)
            act_.dma_start(rw[:, :], router_w[:, :]).then_inc(small_in, 16)
            act_.dma_start(b_cols[:, 0:1], wq_b.rearrange("(d o) -> d o", o=1)).then_inc(small_in, 16)
            act_.dma_start(b_cols[:, 1:2], wk_b.rearrange("(d o) -> d o", o=1)).then_inc(small_in, 16)
            act_.wait_ge(wT_done, 1)
            act_.activation(w_T[:, :, :], bank_x[:, :].rearrange("p (n d) -> p n d", n=4), ACT.Copy).then_inc(wT_kept, 1)

            def normalise_x(g):
                if is_first(g):
                    act_.wait_ge(x_stats, 1)
                else:
                    act_.wait_ge(xlnT_done, g)
                    act_.wait_ge(q_bo_ready, g)
                for j in range(GB):
                    last = act_.activation(xln[:, j, :], x_all[:, bass.ds(g * (GB * D) + j * D, D)], ACT.Identity,
                                           bias=x_nb[:, bass.ds(g * GB + j, 1)], scale=x_rstd[:, bass.ds(g * GB + j, 1)])
                last.then_inc(xln_ready, 1)

            def keep_q(g):
                act_.wait_ge(xlnT_done, g + 1)
                act_.activation(xlnT[:, :], bank_x[:, 0:GB * S], ACT.Copy).then_inc(xlnT_kept, 1)
                act_.wait_ge(q_done, g + 1)
                if is_first(g):
                    act_.wait_ge(consts_ready, 1)
                act_.activation(qT[:, :], bank_q[:, 0:GB * S], ACT.Identity, bias=bq_dk[:, 0:1], scale=1.0 / DK).then_inc(q_kept, 1)

            def keep_gram(g, pair):
                act_.wait_ge(gram_done, GB * g + 2 * pair + 2)
                act_.activation(gram[:, 2 * pair:2 * pair + 2, :],
                                bank_g[pair][:, 0:2 * CW].rearrange("p (j d) -> p j d", j=2), ACT.Copy).then_inc(gram_kept, 1)

            def column_sums(h):
                act_.wait_ge(gram_kept, 2 * (h + 1))
                if is_first(h):
                    act_.wait_ge(small_in, 16 * 9)
                else:
                    act_.wait_ge(u_kept, h)
                for j in range(GB):
                    last = act_.activation(s_bk[:, j, :], bk_rows[:, :], ACT.Identity, scale=gram[:, j, D:CW])
                last.then_inc(s_bk_ready, 1)

            def keep_c(h):
                act_.wait_ge(c_done, h + 1)
                act_.activation(ctxT[:, :], bank_c[:, 0:GB * S], ACT.Copy).then_inc(c_kept, 1)

            def keep_hT(h):
                act_.wait_ge(hT_done, h + 1)
                act_.activation(hT[:, :], bank_m[:, 0:GB * S], ACT.Copy).then_inc(hT_kept, 1)

            def tanh(h):
                act_.wait_ge(below_ready, h + 1)
                act_.activation(th[:, :, :], below[:, :, :], ACT.Tanh, scale=0.5).then_inc(th_ready, 1)

            normalise_x(0)
            keep_gram(0, 0)
            keep_q(0)
            keep_gram(0, 1)

            def round_of(g):
                column_sums(g - 1)
                normalise_x(g)
                keep_c(g - 1)
                keep_gram(g, 0)
                keep_q(g)
                keep_hT(g - 1)
                tanh(g - 1)
                keep_gram(g, 1)

            round_of(1)
            with act_.Fori(2, NG) as g:
                round_of(g)
            column_sums(NG - 1)
            keep_c(NG - 1)
            keep_hT(NG - 1)
            tanh(NG - 1)

            def keep_h2T(t, slot):
                act_.wait_ge(h2T_done, t + 1)
                if not (isinstance(t, int) and t < 2):
                    act_.wait_ge(g_done, t - 1)
                act_.activation(h2T[:, slot, :], bank_x[:, 0:P], ACT.Copy).then_inc(h2T_kept, 1)

            def silu(t, slot):
                act_.wait_ge(a_done, t + 1)
                if not (isinstance(t, int) and t < 2):
                    act_.wait_ge(act_ready, t - 1)
                act_.activation(gate_s[:, slot, :], bank_g[0][:, :], ACT.Silu).then_inc(silu_done, 1)

            keep_h2T(0, 0)
            silu(0, 0)
            keep_h2T(1, 1)
            silu(1, 1)
            keep_h2T(2, 0)
            with act_.Fori(1, TILES // 2 - 1) as i:
                silu(2 * i, 0)
                keep_h2T(2 * i + 1, 1)
                silu(2 * i + 1, 1)
                keep_h2T(2 * i + 2, 0)
            silu(TILES - 2, 0)
            keep_h2T(TILES - 1, 1)
            silu(TILES - 1, 1)

        @block.vector
        def _(v):
            step = Steps(v, dve)

            def rsqrt(variance, n, final, last_sem=None):
                step.done(v.tensor_scalar(ve[:, 0:n], variance, LN_EPS, None, ALU.add))
                step.then()
                step.done(v.tensor_scalar(y0[:, 0:n].bitcast(I32), ve[:, 0:n].bitcast(I32), -0.5, GUESS, ALU.mult, ALU.add))
                step.done(v.tensor_scalar(half[:, 0:n], ve[:, 0:n], -0.5, None, ALU.mult))
                step.then()
                for k in range(NEWTON_STEPS):
                    step.done(v.tensor_tensor(sq[:, 0:n], y0[:, 0:n], y0[:, 0:n], ALU.mult))
                    step.then()
                    step.done(v.tensor_tensor(sq[:, 0:n], sq[:, 0:n], half[:, 0:n], ALU.mult))
                    step.then()
                    dst = final if k == NEWTON_STEPS - 1 else y0[:, 0:n]
                    step.done(v.scalar_tensor_tensor(out=dst, in0=sq[:, 0:n], scalar=1.5, in1=y0[:, 0:n],
                                                     op0=ALU.add, op1=ALU.mult))
                    step.then()

            for e in range(E):
                step.done(v.memset(first_w[:, :, e], float(E - e)))
            v.wait_ge(x_in, 16)
            for b in range(B):
                step.done(v.bn_stats(stats[:, b, :], x_all[:, b * D:(b + 1) * D]))
            step.then()
            for b in range(B):
                step.done(v.bn_aggr(mv[:, b, :], stats[:, b, :]))
            step.then()
            rsqrt(mv[:, :, 1], B, x_rstd[:, :])
            v.scalar_tensor_tensor(out=x_nb[:, :], in0=mv[:, :, 0], scalar=-1.0, in1=x_rstd[:, :],
                                   op0=ALU.mult, op1=ALU.mult).then_inc(x_stats, 1)
            v.wait_ge(small_in, 16 * 9)
            v.wait_ge(pool_set, 17)
            step.done(v.tensor_scalar(bq_dk[:, :], b_cols[:, 0:1], 1.0 / DK, None, ALU.mult))
            step.done(v.tensor_scalar(bk_s2[:, :], b_cols[:, 1:2], float(S2), None, ALU.mult))
            step.done(v.tensor_copy(region[:, :], next_i[:, :]))
            step.done(v.tensor_copy(next_free[:, :], next_i[:, :]))
            step.done(v.tensor_copy(stair[:, :], stair_i[:, :]))
            step.done(v.tensor_copy(tile_no[:, :], tile_i[:, :]))
            step.done(v.tensor_copy(e_no[:, :], e_i[:, :]))
            v.tensor_tensor(bv_mask[:, :], bv_rows[:, :], head_mask[:, :], ALU.mult).then_inc(consts_ready, 1)
            step.then()
            setup_steps = step.count

            def per_row(a):
                return a.unsqueeze(2).to_broadcast([S, GB, E])

            def layer_norm_stats(src, final, between):
                for j in range(GB):
                    step.done(v.bn_stats(stats[:, j, :], src[:, j, 0:D]))
                step.then()
                step.done(between())
                for j in range(GB):
                    step.done(v.bn_aggr(mv[:, j, :], stats[:, j, :]))
                step.then()
                rsqrt(mv[:, 0:GB, 1], GB, final)

            STEPS_PER_GROUP = 65

            def chain(h):
                start = is_first(h)
                step.begin(setup_steps + STEPS_PER_GROUP * h)
                v.wait_ge(w_done, h + 1)
                v.tensor_scalar(w4[:, :], ps_w, bk_s2[:, 0:1], None, ALU.add).then_inc(w4_ready, 1)
                v.wait_ge(u_done, h + 1)
                v.wait_ge(s_bk_ready, h + 1)
                v.tensor_tensor(u_sb[:, :, :], bank_u[:, :].rearrange("p (j d) -> p j d", j=GB), s_bk[:, :, :],
                                ALU.add).then_inc(u_kept, 1)
                v.wait_ge(m_done, h + 1)
                step.done(v.tensor_tensor(m_own[:, :, :], bank_m[:, :].rearrange("p (j d) -> p j d", j=GB),
                                          head_mask[:, :].unsqueeze(1).to_broadcast([P, GB, D]), ALU.mult))
                v.wait_ge(w_bv_ready, h + 1)
                step.then()
                v.tensor_tensor(m_sb[:, :, :], m_own[:, :, :], w_bv[:, :, :], ALU.add).then_inc(m_kept, 1)
                v.wait_ge(mask_in, 16 * (h + 1))
                v.tensor_reduce(masked[:, :], mask_sb[:, :, :].bitcast(I32), AX, ALU.max).then_inc(mask_used, 1)
                v.wait_ge(mask_used, h + 1)
                v.wait_ge(o_done, h + 1)
                v.wait_ge(q_bo_ready, h + 1)
                v.tensor_tensor(res[:, :, :], bank_u[0:S, :].rearrange("p (j d) -> p j d", j=GB), q_bo[:, :, :],
                                ALU.add).then_inc(res_ready, 1)
                v.wait_ge(res_ready, h + 1)
                layer_norm_stats(res, y0[:, 0:GB], lambda: v.tensor_scalar(
                    nan_or_0[:, :], masked[:, :], 0.0, NAN_BITS, ALU.is_gt, ALU.mult))
                for j in range(GB):
                    step.done(v.tensor_scalar(nrm[:, j, :], res[:, j, :], mv[:, j, 0:1], y0[:, j:j + 1],
                                              ALU.subtract, ALU.mult))
                step.then()
                step.done(v.tensor_tensor(nrm[:, :, :], nrm[:, :, :], g_rows[:, :].unsqueeze(1).to_broadcast([S, GB, D]),
                                          ALU.mult))
                v.wait_ge(x_b_ready, h + 1)
                if not start:
                    v.wait_ge(rows_out, 16 * h)
                    v.wait_ge(map_out, 16 * GB * h)
                step.then()
                v.tensor_tensor(rows[:, :, 0:D], nrm[:, :, :], x_b[:, :, :], ALU.add).then_inc(x1_ready, 1)
                v.wait_ge(x1_ready, h + 1)
                layer_norm_stats(rows, rows[:, :, RSTD], lambda: v.tensor_scalar(
                    row_no[:, :], row_no[:, :], float(GB * S), None, ALU.add))
                step.done(v.tensor_copy(rows[:, :, MEAN], mv[:, 0:GB, 0]))
                for j in range(GB):
                    last = v.tensor_scalar(h_sb[:, j, :], rows[:, j, 0:D], mv[:, j, 0:1], rows[:, j, RSTD:RSTD + 1],
                                           ALU.subtract, ALU.mult)
                last.then_inc(h_ready, 1)
                v.wait_ge(logit_done, h + 1)
                step.done(v.tensor_tensor(logit[:, :, :], ps_logit.rearrange("p (j e) -> p j e", j=GB),
                                          rb_rows[:, :].unsqueeze(1).to_broadcast([S, GB, E]), ALU.add))
                step.then()
                step.done(v.tensor_reduce(best[:, :], logit[:, :, :], AX, ALU.max))
                step.then()
                v.tensor_tensor(below[:, :, :], logit[:, :, :], per_row(best[:, :]), ALU.subtract).then_inc(below_ready, 1)
                v.wait_ge(below_ready, h + 1)
                step.done(v.scalar_tensor_tensor(out=score[:, :, :], in0=below[:, :, :], scalar=0.0, in1=first_w[:, :, :],
                                                 op0=ALU.is_ge, op1=ALU.mult))
                step.then()
                step.done(v.tensor_reduce(best[:, :], score[:, :, :], AX, ALU.max))
                step.then()
                v.tensor_tensor(choice[:, :, :], score[:, :, :], per_row(best[:, :]), ALU.is_equal).then_inc(choice_ready, 1)
                v.wait_ge(th_ready, h + 1)
                step.done(v.tensor_scalar(e1[:, :, :], th[:, :, :], -1.0, 1.0, ALU.mult, ALU.add))
                step.then()
                step.done(v.reciprocal(e2[:, :, :], e1[:, :, :]))
                step.then()
                step.done(v.scalar_tensor_tensor(out=e3[:, :, :], in0=th[:, :, :], scalar=1.0, in1=e2[:, :, :],
                                                 op0=ALU.add, op1=ALU.mult))
                step.then()
                step.done(v.tensor_reduce(esum[:, :], e3[:, :, :], AX, ALU.add))
                step.then()
                step.done(v.reciprocal(esum[:, :], esum[:, :]))
                v.wait_ge(rank_done, h + 1)
                step.done(v.tensor_tensor(rank[:, :, :], ps_rank.rearrange("p (j e) -> p j e", j=GB),
                                          next_free[0:S, :].unsqueeze(1).to_broadcast([S, GB, E]), ALU.add))
                step.then()
                step.done(v.tensor_tensor(rows[:, :, GATE], esum[:, :], nan_or_0[:, :].bitcast(F32), ALU.add))
                step.done(v.tensor_tensor(rank[:, :, :], rank[:, :, :], choice[:, :, :], ALU.mult))
                v.tensor_tensor(next_free[:, :], next_free[:, :], ps_count, ALU.add).then_inc(rank_kept, 1)
                step.then()
                v.wait_ge(rank_kept, h + 1)
                step.done(v.tensor_reduce(pos[:, :], rank[:, :, :], AX, ALU.add))
                step.then()
                step.done(v.tensor_copy(pos_i[:, :], pos[:, :]))
                step.then()
                step.done(v.tensor_single_scalar(low[:, :], pos_i[:, :], P - 1, ALU.bitwise_and))
                step.done(v.tensor_single_scalar(high[:, :], pos_i[:, :], P.bit_length() - 1, ALU.logical_shift_right))
                step.then()
                v.scalar_tensor_tensor(out=map_i[:, :], in0=low[:, :], scalar=float(COLS), in1=high[:, :],
                                       op0=ALU.mult, op1=ALU.add).then_inc(rows_ready, 1)
                assert step.count == STEPS_PER_GROUP, step.count


            chain(0)
            with v.Fori(1, NG) as h:
                chain(h)

            step.begin(setup_steps + STEPS_PER_GROUP * NG)

            def over_t(a):
                return a.unsqueeze(1).to_broadcast([P, TILES, E])

            def over_e(a):
                return a.unsqueeze(2).to_broadcast([P, TILES, E])

            step.done(v.tensor_tensor(count[:, :], next_free[:, :], region[:, :], ALU.subtract))
            step.then()
            step.done(v.tensor_tensor(more[:, :, :], count[:, :].unsqueeze(2).to_broadcast([P, E, NT_MAX]),
                                      stair[:, :].unsqueeze(1).to_broadcast([P, E, NT_MAX]), ALU.is_gt))
            step.then()
            step.done(v.tensor_reduce(nt[:, :], more[:, :, :], AX, ALU.add))
            step.then()
            step.done(v.tensor_tensor(nt_all[:, :, :], nt[:, :].unsqueeze(1).to_broadcast([P, E, E]), upto[:, :, :],
                                      ALU.mult))
            step.then()
            step.done(v.tensor_reduce(end[:, :], nt_all[:, :, :], AX, ALU.add))
            step.then()
            step.done(v.tensor_tensor(first[:, :], end[:, :], nt[:, :], ALU.subtract))
            step.done(v.tensor_tensor(own_b[:, :, :], over_e(tile_no[:, :]), over_t(end[:, :]), ALU.is_lt))
            step.then()
            step.done(v.tensor_tensor(own_a[:, :, :], over_e(tile_no[:, :]), over_t(first[:, :]), ALU.is_ge))
            step.done(v.scalar_tensor_tensor(out=from_e[:, :], in0=region[:, :], scalar=1.0 / P, in1=first[:, :],
                                             op0=ALU.mult, op1=ALU.subtract))
            step.then()
            step.done(v.tensor_tensor(own[:, :, :], own_a[:, :, :], own_b[:, :, :], ALU.mult))
            step.done(v.scalar_tensor_tensor(out=col_te[:, :, :], in0=over_e(tile_no[:, :]), scalar=-float(COLS),
                                             in1=over_t(from_e[:, :]), op0=ALU.add, op1=ALU.add))
            step.then()
            step.done(v.tensor_tensor(pick[:, 0, :, :], own[:, :, :], over_t(e_no[:, :]), ALU.mult))
            step.done(v.tensor_tensor(pick[:, 1, :, :], own[:, :, :], col_te[:, :, :], ALU.mult))
            step.then()
            step.done(v.tensor_reduce(picked[:, :, :], pick[:, :, :, :], AX, ALU.add))
            step.then()
            v.tensor_copy(expert_i[:, :], picked[:, 0, :])
            v.tensor_scalar(col_i[:, :], picked[:, 1, :], float(COLS), None, ALU.add).then_inc(table_ready, 1)

            def at(t, column, n):
                return slots[:, bass.ds(t * ROW + column, n)]

            def normalise(t, slot, i):
                v.wait_ge(gathered[slot], 16 * (i + 1))
                if not (isinstance(t, int) and t < 2):
                    v.wait_ge(h2T_done, t - 1)
                v.tensor_scalar(h2[:, slot, :], at(t, 0, D), at(t, MEAN, 1), at(t, RSTD, 1),
                                ALU.subtract, ALU.mult).then_inc(h2_ready, 1)

            def keep_actT(t, slot):
                v.wait_ge(actT_done, t + 1)
                v.tensor_copy(actT[:, slot, :], bank_c[:, :]).then_inc(actT_kept, 1)

            def product(t, slot):
                v.wait_ge(silu_done, t + 1)
                v.wait_ge(g_done, t + 1)
                v.tensor_tensor(act[:, slot, :], gate_s[:, slot, :], bank_g[1][:, :], ALU.mult).then_inc(act_ready, 1)

            def finish(t, slot, i):
                v.wait_ge(y_done, t + 1)
                if not (isinstance(t, int) and t < 2):
                    v.wait_ge(out_written[slot], 16 * i)
                v.scalar_tensor_tensor(out=out_sb[:, slot, :], in0=bank_u[:, 0:D], scalar=at(t, GATE, 1), in1=at(t, 0, D),
                                       op0=ALU.mult, op1=ALU.add).then_inc(out_ready, 1)

            normalise(0, 0, 0)
            normalise(1, 1, 0)
            product(0, 0)
            normalise(2, 0, 1)
            keep_actT(0, 0)
            product(1, 1)
            finish(0, 0, 0)
            normalise(3, 1, 1)

            def two_tiles(i):
                for k in range(2):
                    t = 2 * i + k
                    keep_actT(t - 1, 1 - k)
                    product(t, k)
                    finish(t - 1, 1 - k, i - 1 + k)
                    normalise(t + 2, k, i + 1)

            two_tiles(1)
            with v.Fori(2, TILES // 2 - 1) as i:
                two_tiles(i)
            for t in (TILES - 2, TILES - 1):
                keep_actT(t - 1, (t - 1) % 2)
                product(t, t % 2)
                finish(t - 1, (t - 1) % 2, (t - 1) // 2)
            keep_actT(TILES - 1, 1)
            finish(TILES - 1, 1, (TILES - 1) // 2)

        @block.tensor
        def _(pe):
            pe.wait_ge(w_in, 64)
            pe.wait_ge(ident_set, 1)
            for n in range(4):
                last = pe.transpose(bank_x[:, n * D:(n + 1) * D], w_raw[:, n, :], ident[:, :])
            last.then_inc(wT_done, 1)
            wkT, wvT, wqT, woT = w_T[:, 1, :], w_T[:, 2, :], w_T[:, 0, :], w_T[:, 3, :]

            def gram_of(g, j, between=()):
                between = dict(between)
                pe.wait_ge(ctx_in[j], 32 * (g + 1))
                if not is_first(g) and j % 2 == 0:
                    pe.wait_ge(gram_kept, 2 * (g - 1) + j // 2 + 1)
                to = bank_g[j // 2][:, (j % 2) * CW:(j % 2 + 1) * CW]
                for c in range(NCH):
                    last = pe.matmul(to, ctx_sb[:, j, c, 0:D], ctx_sb[:, j, c, :], start=(c == 0), stop=(c == NCH - 1))
                    if c in between:
                        for stage, of in between[c]:
                            stage(of)
                last.then_inc(gram_done, 1)

            def u_of(h):
                pe.wait_ge(gram_kept, 2 * (h + 1))
                if is_first(h):
                    pe.wait_ge(wT_kept, 1)
                else:
                    pe.wait_ge(res_ready, h)
                for j in range(GB):
                    last = pe.matmul(bank_u[:, j * D:(j + 1) * D], gram[:, j, 0:D], wkT, start=True, stop=True)
                last.then_inc(u_done, 1)

            def w_of(h):
                if not is_first(h):
                    pe.wait_ge(rank_kept, h)
                pe.matmul(ps_w, wkT, gram[:, :, D], start=True, stop=True).then_inc(w_done, 1)

            def m_of(h):
                pe.wait_ge(u_kept, h + 1)
                if not is_first(h):
                    pe.wait_ge(hT_kept, h)
                for j in range(GB):
                    last = pe.matmul(bank_m[:, j * D:(j + 1) * D], u_sb[:, j, :], wvT, start=True, stop=True)
                last.then_inc(m_done, 1)

            def c_of(h):
                pe.wait_ge(m_kept, h + 1)
                pe.wait_ge(q_kept, h + 1)
                for j in range(GB):
                    last = pe.matmul(bank_c[:, j * S:(j + 1) * S], m_sb[:, j, :], qT[:, j * S:(j + 1) * S],
                                     start=True, stop=True)
                last.then_inc(c_done, 1)

            def o_of(h):
                pe.wait_ge(c_kept, h + 1)
                for j in range(GB):
                    last = pe.matmul(bank_u[0:S, j * D:(j + 1) * D], ctxT[:, j * S:(j + 1) * S], woT,
                                     start=True, stop=True)
                last.then_inc(o_done, 1)

            def xT_of(g):
                pe.wait_ge(xln_ready, g + 1)
                if is_first(g):
                    pe.wait_ge(wT_kept, 1)
                else:
                    pe.wait_ge(xlnT_kept, g)
                for j in range(GB):
                    last = pe.transpose(bank_x[:, j * S:(j + 1) * S], xln[:, j, :], ident[0:S, 0:S])
                last.then_inc(xlnT_done, 1)

            def q_of(g):
                pe.wait_ge(xlnT_kept, g + 1)
                if not is_first(g):
                    pe.wait_ge(q_kept, g)
                pe.matmul(bank_q[:, 0:GB * S], wqT, xlnT[:, :], start=True, stop=True).then_inc(q_done, 1)

            def hT_of(h):
                pe.wait_ge(h_ready, h + 1)
                for j in range(GB):
                    last = pe.transpose(bank_m[:, j * S:(j + 1) * S], h_sb[:, j, :], ident[0:S, 0:S])
                last.then_inc(hT_done, 1)

            def logits_of(h):
                pe.wait_ge(hT_kept, h + 1)
                if is_first(h):
                    pe.wait_ge(small_in, 16 * 9)
                for j in range(GB):
                    last = pe.matmul(ps_logit[:, j * E:(j + 1) * E], hT[:, j * S:(j + 1) * S], rw[:, :],
                                     start=True, stop=True)
                last.then_inc(logit_done, 1)

            def ranks_of(h):
                pe.wait_ge(choice_ready, h + 1)
                if is_first(h):
                    pe.wait_ge(pool_set, 9)
                pe.matmul(ps_rank, before[:, :], choice[:, :, :].rearrange("q j e -> q (j e)"), start=True, stop=False)
                for j in range(GB - 1):
                    n = GB - 1 - j
                    pe.matmul(ps_rank[:, (j + 1) * E:].rearrange("q (n e) -> q n e", n=n), ones[:, 0:S],
                              choice[:, j:j + 1, :].to_broadcast([S, n, E]), start=False, stop=(n == 1))
                for j in range(GB):
                    last = pe.matmul(ps_count, ones[:, :], choice[:, j, :], start=(j == 0), stop=(j == GB - 1))
                last.then_inc(rank_done, 1)

            gram_of(0, 0)
            gram_of(0, 1)
            xT_of(0)
            gram_of(0, 2, {NCH // 2: [(q_of, 0)]})
            gram_of(0, 3)

            def round_of(g):
                gram_of(g, 0, {1: [(u_of, g - 1), (w_of, g - 1)], 4: [(m_of, g - 1)], 8: [(c_of, g - 1)],
                               11: [(o_of, g - 1)]})
                gram_of(g, 1)
                xT_of(g)
                gram_of(g, 2, {NCH // 2: [(q_of, g)]})
                gram_of(g, 3, {6: [(hT_of, g - 1)], 10: [(logits_of, g - 1)]})
                ranks_of(g - 1)

            round_of(1)
            with pe.Fori(2, NG) as g:
                round_of(g)
            for stage in (u_of, w_of, m_of, c_of, o_of, hT_of, logits_of, ranks_of):
                stage(NG - 1)

            def h2T_of(t, slot):
                pe.wait_ge(h2_ready, t + 1)
                if not is_first(t):
                    pe.wait_ge(h2T_kept, t)
                pe.transpose(bank_x[:, 0:P], h2[:, slot, :], ident[:, :]).then_inc(h2T_done, 1)

            def up(t, slot, part_, expert):
                if part_ == 0:
                    pe.wait_ge(h2T_kept, t + 1)
                if not is_first(t):
                    pe.wait_ge(*((silu_done, t) if part_ == 0 else (act_ready, t)))
                pe.matmul(bank_g[part_][:, :], h2T[:, slot, :], w1_sb[:, bass.ds(expert * F2 + part_ * FF, FF)],
                          start=True, stop=True).then_inc((a_done, g_done)[part_], 1)

            def actT_of(t, slot):
                pe.wait_ge(act_ready, t + 1)
                if not is_first(t):
                    pe.wait_ge(actT_kept, t)
                for c in range(FC):
                    last = pe.transpose(bank_c[:, c * P:(c + 1) * P], act[:, slot, c * P:(c + 1) * P], ident[:, :])
                last.then_inc(actT_done, 1)

            def down(t, slot, expert):
                pe.wait_ge(actT_kept, t + 1)
                if not is_first(t):
                    pe.wait_ge(out_ready, t)
                for c in range(FC):
                    last = pe.matmul(bank_u[:, 0:D], actT[:, slot, c * P:(c + 1) * P],
                                     w2_sb[:, bass.ds(expert * (FC * D) + c * D, D)], start=(c == 0), stop=(c == FC - 1))
                last.then_inc(y_done, 1)

            def expert_of(t):
                return pe.value_load(expert_i[0:1, bass.ds(t, 1)], min_val=0, max_val=E - 1)

            pe.wait_ge(table_ready, 1)
            pe.wait_ge(w1_in, 16 * E)
            pe.wait_ge(w2_in, 16 * E)
            h2T_of(0, 0)
            here = expert_of(0)
            up(0, 0, 0, here)
            h2T_of(1, 1)
            up(0, 0, 1, here)

            def tile(t, slot):
                here = expert_of(t)
                up(t, slot, 0, here)
                if not (isinstance(t, int) and t == TILES - 1):
                    h2T_of(t + 1, 1 - slot)
                actT_of(t - 1, 1 - slot)
                up(t, slot, 1, here)
                down(t - 1, 1 - slot, expert_of(t - 1))

            tile(1, 1)
            tile(2, 0)
            with pe.Fori(1, TILES // 2 - 1) as i:
                tile(2 * i + 1, 1)
                tile(2 * i + 2, 0)
            tile(TILES - 1, 1)
            actT_of(TILES - 1, 1)
            down(TILES - 1, 1, expert_of(TILES - 1))


def kernel(**inputs):
    import concourse.bacc as bacc
    import numpy as np
    from concourse.bass_utils import run_bass_kernel_spmd

    names = ("x", "ctx_1024", "mask_Bx1xSxS2_bf0", "L0_xattn_wq_w", "L0_xattn_wq_b", "L0_xattn_wk_w", "L0_xattn_wk_b",
             "L0_xattn_wv_w", "L0_xattn_wv_b", "L0_xattn_wo_w", "L0_xattn_wo_b", "L0_xattn_ln_g", "L0_xattn_ln_b",
             "L0_ffn_router_w", "L0_ffn_router_b", "L0_ffn_w1", "L0_ffn_w2")
    nc = bacc.Bacc("TRN2", target_bir_lowering=False, num_devices=1)
    arrays, args = {}, []
    for name in names:
        a = np.ascontiguousarray(inputs[name])
        arrays[name] = a
        args.append(nc.dram_tensor(name, a.shape, mybir.dt.from_np(a.dtype), kind="ExternalInput").ap())
    out = nc.dram_tensor("out", arrays["x"].shape, F32, kind="ExternalOutput").ap()
    build(nc, *args, out)
    return run_bass_kernel_spmd(nc, [arrays], core_ids=[0]).results[0]["out"]
```

```python
from contextlib import ExitStack

import concourse.bass as bass
from concourse import mybir

ALU = mybir.AluOpType
ACT = mybir.ActivationFunctionType
AX = mybir.AxisListType.X
F32 = mybir.dt.float32
BF16 = mybir.dt.bfloat16
I32 = mybir.dt.int32
U8 = mybir.dt.uint8

P = 128
LN_EPS = 1e-5
HEADS = 16
DK = 2.828125
NAN_BITS = 2143289344.0
SKIP = 1000000


class Steps:

    def __init__(self, engine, semaphore):
        self.engine, self.semaphore, self.base, self.count = engine, semaphore, 0, 0

    def begin(self, base):
        self.base, self.count = base, 0

    def done(self, instruction):
        instruction.then_inc(self.semaphore, 1)
        self.count += 1

    def then(self):
        self.engine.wait_ge(self.semaphore, self.base + self.count)


def build(nc, x, ctx_rows, mask, wq_w, wq_b, wk_w, wk_b, wv_w, wv_b, wo_w, wo_b, ln_g, ln_b,
          router_w, router_b, w1, w2, out):
    B, S, D = x.shape
    S2 = ctx_rows.shape[1]
    E, _, F2 = w1.shape
    FF = F2 // 2
    HD = D // HEADS
    assert D == P and HD == 8 and FF % P == 0

    GB = 4
    NG = B // GB
    FULL = S2 // P
    REST = S2 - FULL * P
    NCH = FULL + 1
    CW = D + 1
    TOKENS = B * S
    TILES = (TOKENS + E * (P - 1)) // P
    ROW = D + 3
    MEAN, RSTD, GATE = D, D + 1, D + 2
    FC = FF // P
    MW = S2 // 4
    NT_MAX = (TOKENS + P - 1) // P
    COLS = E * NT_MAX

    token_rows = nc.dram_tensor("token_rows", (TOKENS, ROW), F32, kind="Internal").ap()
    slot_map = nc.dram_tensor("slot_map", (P * COLS, 1), I32, kind="Internal").ap()
    out_rows = out.rearrange("b s d -> (b s) d")

    with ExitStack() as stack:
        def sb(name, shape, dtype=F32):
            return stack.enter_context(nc.sbuf_tensor(name, shape, dtype))

        def bank(name, shape):
            return stack.enter_context(nc.psum_tensor(name, shape, F32))

        def sem(name):
            return stack.enter_context(nc.semaphore(name))

        x_all = sb("x_all", [S, B * D])
        w_raw = sb("w_raw", [P, 4, D])
        w_T = sb("w_T", [P, 4, D])
        bk_rows = sb("bk_rows", [P, D])
        bv_rows = sb("bv_rows", [P, D])
        bo_rows = sb("bo_rows", [S, D])
        g_rows = sb("g_rows", [S, D])
        b_rows = sb("b_rows", [S, D])
        rb_rows = sb("rb_rows", [S, E])
        rw = sb("rw", [P, E])
        b_cols = sb("b_cols", [P, 2])
        bq_dk = sb("bq_dk", [P, 1])
        bk_s2 = sb("bk_s2", [P, 1])
        w1_sb = sb("w1_sb", [P, E * F2])
        w2_sb = sb("w2_sb", [P, E * FC * D])
        ident = sb("ident", [P, P])
        head_mask = sb("head_mask", [P, D])
        bv_mask = sb("bv_mask", [P, D])
        before = sb("before", [S, S], BF16)
        ones = sb("ones", [S, P], BF16)
        first_w = sb("first_w", [S, GB, E])

        ctx_sb = sb("ctx_sb", [P, GB, NCH, CW])
        gram = sb("gram", [P, GB, CW])
        s_bk = sb("s_bk", [P, GB, D])
        w4 = sb("w4", [P, GB])
        w_bv = sb("w_bv", [P, GB, D])
        u_sb = sb("u_sb", [P, GB, D])
        m_own = sb("m_own", [P, GB, D])
        m_sb = sb("m_sb", [P, GB, D])
        xln = sb("xln", [S, GB, D])
        xlnT = sb("xlnT", [P, GB * S])
        qT = sb("qT", [P, GB * S])
        ctxT = sb("ctxT", [P, GB * S])
        q_bo = sb("q_bo", [S, GB, D])
        x_b = sb("x_b", [S, GB, D])
        res = sb("res", [S, GB, D])
        nrm = sb("nrm", [S, GB, D])
        rows = sb("rows", [S, B, ROW])
        h_sb = sb("h_sb", [S, GB, D])
        hT = sb("hT", [P, GB * S])
        stats = sb("stats", [S, B, 6])
        mv = sb("mv", [S, B, 2])
        ve = sb("ve", [S, B])
        std = sb("std", [S, B])
        half = sb("half", [S, B])
        y0 = sb("y0", [S, B])
        unused = sb("unused", [S, 1])
        sq = sb("sq", [S, B])
        x_rstd = sb("x_rstd", [S, B])
        x_nb = sb("x_nb", [S, B])
        mask_sb = sb("mask_sb", [S, GB, S2], U8)
        masked = sb("masked", [S, B])
        nan_or_0 = sb("nan_or_0", [S, B], I32)

        logit = sb("logit", [S, GB, E])
        below = sb("below", [S, B, E])
        best = sb("best", [S, GB])
        score = sb("score", [S, GB, E])
        choice = sb("choice", [S, GB, E], BF16)
        th = sb("th", [S, B, E])
        e1 = sb("e1", [S, B, E])
        e2 = sb("e2", [S, B, E])
        e3 = sb("e3", [S, B, E])
        esum = sb("esum", [S, B])
        e_inv = sb("e_inv", [S, B])
        r_rstd = sb("r_rstd", [S, GB])
        rank = sb("rank", [S, GB, E])
        pos = sb("pos", [S, GB])
        pos_i = sb("pos_i", [S, GB], I32)
        low = sb("low", [S, GB], I32)
        high = sb("high", [S, GB], I32)
        map_i = sb("map_i", [S, GB], I32)
        next_i = sb("next_i", [P, E], I32)
        region = sb("region", [P, E])
        next_free = sb("next_free", [P, E])
        row_no = sb("row_no", [S, GB], I32)

        count = sb("count", [P, E])
        stair_i = sb("stair_i", [P, NT_MAX], I32)
        stair = sb("stair", [P, NT_MAX])
        tile_i = sb("tile_i", [P, TILES], I32)
        tile_no = sb("tile_no", [P, TILES])
        e_i = sb("e_i", [P, E], I32)
        e_no = sb("e_no", [P, E])
        upto = sb("upto", [P, E, E])
        more = sb("more", [P, E, NT_MAX])
        nt = sb("nt", [P, E])
        nt_all = sb("nt_all", [P, E, E])
        end = sb("end", [P, E])
        first = sb("first", [P, E])
        own_a = sb("own_a", [P, TILES, E])
        own_b = sb("own_b", [P, TILES, E])
        own = sb("own", [P, TILES, E])
        pick = sb("pick", [P, 2, TILES, E])
        from_e = sb("from_e", [P, E])
        col_te = sb("col_te", [P, TILES, E])
        picked = sb("picked", [P, 2, TILES])
        col_i = sb("col_i", [P, TILES], I32)
        expert_i = sb("expert_i", [P, TILES], I32)

        map_sb = sb("map_sb", [P, COLS + 1], I32)
        token = sb("token", [P, TILES], I32)
        slots = sb("slots", [P, TILES * ROW])
        h2 = sb("h2", [P, 2, D])
        h2T = sb("h2T", [P, 2, P])
        gate_s = sb("gate_s", [P, 2, FF])
        act = sb("act", [P, 2, FF])
        actT = sb("actT", [P, 2, FF])
        out_sb = sb("out_sb", [P, 2, D])

        bank_g = [bank("bank_g0", [P, 512]), bank("bank_g1", [P, 512])]
        bank_c, bank_u, bank_m = bank("bank_c", [P, 512]), bank("bank_u", [P, 512]), bank("bank_m", [P, 512])
        bank_x, bank_q, bank_r = bank("bank_x", [P, 512]), bank("bank_q", [P, 512]), bank("bank_r", [P, 512])
        ps_w = bank_c[:, GB * S:GB * S + GB]
        ps_logit = bank_r[0:S, 64:64 + GB * E]
        ps_rank = bank_r[0:S, 128:128 + GB * E]
        ps_count = bank_r[:, 192:192 + E]

        x_in, w_in, small_in, w1_in, w2_in = sem("x_in"), sem("w_in"), sem("small_in"), sem("w1_in"), sem("w2_in")
        ctx_in = [sem(f"ctx_in{j}") for j in range(GB)]
        mask_in = sem("mask_in")
        ones_set = sem("ones_set")
        pool_set = sem("pool_set")
        ident_set = sem("ident_set")
        wT_done, wT_kept = sem("wT_done"), sem("wT_kept")
        consts_ready = sem("consts_ready")
        x_var_ready, x_std_ready, x_stats = sem("x_var_ready"), sem("x_std_ready"), sem("x_stats")
        var_ready, std_ready = sem("var_ready"), sem("std_ready")
        gram_done = sem("gram_done")
        gram_kept = sem("gram_kept")
        xln_ready = sem("xln_ready")
        xlnT_done, xlnT_kept = sem("xlnT_done"), sem("xlnT_kept")
        q_done, q_kept = sem("q_done"), sem("q_kept")
        q_bo_ready, x_b_ready = sem("q_bo_ready"), sem("x_b_ready")
        s_bk_ready = sem("s_bk_ready")
        u_done, u_kept = sem("u_done"), sem("u_kept")
        w_done, w4_ready, w_bv_ready = sem("w_done"), sem("w4_ready"), sem("w_bv_ready")
        m_done, m_kept = sem("m_done"), sem("m_kept")
        c_done, c_kept = sem("c_done"), sem("c_kept")
        o_done, res_ready = sem("o_done"), sem("res_ready")
        x1_ready, h_ready = sem("x1_ready"), sem("h_ready")
        hT_done, hT_kept = sem("hT_done"), sem("hT_kept")
        logit_done, below_ready, th_ready = sem("logit_done"), sem("below_ready"), sem("th_ready")
        choice_ready, rank_done, rank_kept = sem("choice_ready"), sem("rank_done"), sem("rank_kept")
        map_i_ready, rows_ready = sem("map_i_ready"), sem("rows_ready")
        mask_used = sem("mask_used")
        map_set = sem("map_set")
        rows_out = sem("rows_out")
        map_out = sem("map_out")
        map_in = sem("map_in")
        token_ready = sem("token_ready")
        dve = sem("dve_step")
        table_ready = sem("table_ready")
        gathered = [sem("gathered0"), sem("gathered1")]
        h2_ready, h2T_done, h2T_kept = sem("h2_ready"), sem("h2T_done"), sem("h2T_kept")
        a_done, silu_done, g_done, act_ready = sem("a_done"), sem("silu_done"), sem("g_done"), sem("act_ready")
        actT_done, actT_kept = sem("actT_done"), sem("actT_kept")
        y_done, out_ready = sem("y_done"), sem("out_ready")
        out_written = [sem("out_written0"), sem("out_written1")]

        block = stack.enter_context(nc.Block())

        def is_first(g):
            return isinstance(g, int) and g == 0

        def wait_alone(engine, semaphore, value, sure, sure_value):
            value = value if isinstance(value, int) else engine.snap(value)
            engine.wait_ge(sure, sure_value)
            engine.wait_ge(semaphore, value)

        def load_group(sp, g):
            for j in range(GB):
                b = g * GB + j
                row = ctx_rows[bass.ds(b, 1)].rearrange("o s d -> (o s) d")
                if is_first(g):
                    sp.wait_ge(ones_set, 1)
                else:
                    wait_alone(sp, gram_done, GB * (g - 1) + j + 1, ones_set, 1)
                sp.dma_start(ctx_sb[:, j, 0:FULL, 0:D],
                             row[0:FULL * P, :].rearrange("(p c) d -> p c d", p=P)).then_inc(ctx_in[j], 16)
                sp.dma_start(ctx_sb[0:REST, j, FULL, 0:D], row[FULL * P:S2, :]).then_inc(ctx_in[j], 16)
            if not is_first(g):
                wait_alone(sp, mask_used, g, ones_set, 1)
            sp.dma_start(mask_sb[:, :, :], mask[bass.ds(g * GB, GB), 0].rearrange("b q k -> q b k")).then_inc(mask_in, 16)

        @block.sync
        def _(sp):
            sp.dma_start(x_all[:, :].rearrange("q (b d) -> q b d", b=B), x.rearrange("b q d -> q b d")).then_inc(x_in, 16)
            load_group(sp, 0)
            with sp.Fori(1, NG) as g:
                load_group(sp, g)
            for e in range(E):
                sp.dma_start(w1_sb[:, e * F2:(e + 1) * F2], w1[e]).then_inc(w1_in, 16)
                sp.dma_start(w2_sb[:, e * FC * D:(e + 1) * FC * D].rearrange("p (c d) -> p c d", c=FC),
                             w2[e].rearrange("(c p) d -> p c d", p=P)).then_inc(w2_in, 16)
            sp.wait_ge(rows_ready, 1)
            sp.dma_start(token_rows.rearrange("(b q) n -> q b n", b=B), rows[:, :, :]).then_inc(rows_out, 16)

        @block.gpsimd
        def _(pool):
            pool.memset(ctx_sb[:, :, FULL, :], 0.0).then_inc(pool_set, 1)
            pool.memset(ident[:, :], 0.0).then_inc(pool_set, 1)
            pool.wait_ge(pool_set, 2)
            pool.memset(ctx_sb[:, :, :, D:CW], 1.0).then_inc(ones_set, 1)
            pool.affine_select(out=ident[:, :], in_=ident[:, :], compare_op=ALU.not_equal, fill=1.0,
                               base=0, pattern=[[-1, P]], channel_multiplier=1).then_inc(ident_set, 1)
            pool.memset(head_mask[:, :], 1.0).then_inc(pool_set, 1)
            pool.memset(before[:, :], 1.0).then_inc(pool_set, 1)
            pool.memset(ones[:, :], 1.0).then_inc(pool_set, 1)
            pool.memset(upto[:, :, :], 1.0).then_inc(pool_set, 1)
            pool.wait_ge(pool_set, 6)
            heads = head_mask[:, :].rearrange("p (h d) -> p h d", d=HD)
            pool.affine_select(out=heads, in_=heads, compare_op=ALU.is_ge, fill=0.0, base=0,
                               pattern=[[-HD, HEADS], [0, HD]], channel_multiplier=1).then_inc(pool_set, 1)
            pool.affine_select(out=before[:, :], in_=before[:, :], compare_op=ALU.is_gt, fill=0.0, base=0,
                               pattern=[[1, S]], channel_multiplier=-1).then_inc(pool_set, 1)
            pool.affine_select(out=upto[:, :, :], in_=upto[:, :, :], compare_op=ALU.is_ge, fill=0.0, base=0,
                               pattern=[[1, E], [-1, E]], channel_multiplier=0).then_inc(pool_set, 1)
            pool.wait_ge(pool_set, 9)
            pool.affine_select(out=heads, in_=heads, compare_op=ALU.is_ge, fill=0.0, base=HD - 1,
                               pattern=[[HD, HEADS], [0, HD]], channel_multiplier=-1).then_inc(pool_set, 1)
            pool.iota(row_no[:, :], pattern=[[S, GB]], base=-GB * S, channel_multiplier=1).then_inc(pool_set, 1)
            pool.iota(next_i[:, :], pattern=[[NT_MAX * P, E]], base=0, channel_multiplier=0).then_inc(pool_set, 1)
            pool.iota(stair_i[:, :], pattern=[[P, NT_MAX]], base=0, channel_multiplier=0).then_inc(pool_set, 1)
            pool.memset(map_sb[:, :], SKIP).then_inc(pool_set, 1)
            pool.iota(tile_i[:, :], pattern=[[1, TILES]], base=0, channel_multiplier=0).then_inc(pool_set, 1)
            pool.iota(e_i[:, :], pattern=[[1, E]], base=0, channel_multiplier=0).then_inc(pool_set, 1)
            pool.memset(slots[:, :], 0.0).then_inc(pool_set, 1)
            pool.wait_ge(pool_set, 17)
            map_2d = slot_map.rearrange("(p c) o -> p (c o)", p=P)
            pool.dma_start(map_2d, map_sb[:, 0:COLS]).then_inc(map_set, 16)
            last_slot = pool.to_reg(P * COLS - 1)
            last_token = pool.to_reg(TOKENS - 1)

            def prepare(g):
                pool.wait_ge(xln_ready, g + 1)
                if not is_first(g):
                    pool.wait_ge(x1_ready, g)
                else:
                    pool.wait_ge(small_in, 16 * 9)
                pool.tensor_tensor(q_bo[:, :, :], xln[:, :, :],
                                   bo_rows[:, :].unsqueeze(1).to_broadcast([S, GB, D]), ALU.add).then_inc(q_bo_ready, 1)
                pool.tensor_tensor(x_b[:, :, :],
                                   x_all[:, bass.ds(g * (GB * D), GB * D)].rearrange("q (b d) -> q b d", b=GB),
                                   b_rows[:, :].unsqueeze(1).to_broadcast([S, GB, D]), ALU.add).then_inc(x_b_ready, 1)

            def outer(h):
                if not is_first(h):
                    pool.wait_ge(m_kept, h)
                else:
                    pool.wait_ge(consts_ready, 1)
                pool.wait_ge(w4_ready, h + 1)
                pool.tensor_tensor(w_bv[:, :, :], bv_mask[:, :].unsqueeze(1).to_broadcast([P, GB, D]),
                                   w4[:, :].unsqueeze(2).to_broadcast([P, GB, D]), ALU.mult).then_inc(w_bv_ready, 1)

            def route(h):
                wait_alone(pool, map_i_ready, h + 1, map_set, 16)
                for j in range(GB):
                    pool.indirect_dma_start(out=slot_map[:, :], out_offset=bass.IndirectOffsetOnAxis(ap=map_i[:, j:j + 1], axis=0),
                                            in_=row_no[:, j:j + 1], in_offset=None, bounds_check=last_slot,
                                            oob_is_err=False).then_inc(map_out, 16)

            prepare(0)
            outer(0)
            prepare(1)
            with pool.Fori(2, NG) as g:
                outer(g - 1)
                route(g - 2)
                prepare(g)
            outer(NG - 1)
            route(NG - 2)
            route(NG - 1)

            AHEAD = 5

            def gather(t):
                column = pool.value_load(col_i[0:1, t:t + 1], min_val=0, max_val=COLS)
                pool.tensor_copy(token[:, t:t + 1], map_sb[:, bass.ds(column, 1)]).then_inc(token_ready, 1)
                if t >= 2:
                    pool.wait_ge(gathered[t % 2], 16 * (t // 2))
                pool.wait_ge(token_ready, t + 1)
                pool.indirect_dma_start(out=slots[:, t * ROW:(t + 1) * ROW], out_offset=None, in_=token_rows[:, :],
                                        in_offset=bass.IndirectOffsetOnAxis(ap=token[:, t:t + 1], axis=0),
                                        bounds_check=last_token, oob_is_err=False).then_inc(gathered[t % 2], 16)

            pool.wait_ge(map_out, 16 * GB * NG)
            pool.dma_start(map_sb[:, 0:COLS], map_2d).then_inc(map_in, 16)
            pool.wait_ge(rows_out, 16)
            pool.wait_ge(map_in, 16)
            pool.wait_ge(table_ready, 1)
            for t in range(AHEAD):
                gather(t)
            for t in range(TILES):
                if t + AHEAD < TILES:
                    gather(t + AHEAD)
                pool.wait_ge(out_ready, t + 1)
                pool.indirect_dma_start(out=out_rows[:, :], out_offset=bass.IndirectOffsetOnAxis(ap=token[:, t:t + 1], axis=0),
                                        in_=out_sb[:, t % 2, :], in_offset=None, bounds_check=last_token,
                                        oob_is_err=False).then_inc(out_written[t % 2], 16)
            pool.wait_ge(out_written[0], 16 * ((TILES + 1) // 2))
            pool.wait_ge(out_written[1], 16 * (TILES // 2))

        @block.scalar
        def _(act_):
            for n, w in enumerate((wq_w, wk_w, wv_w, wo_w)):
                act_.dma_start(w_raw[:, n, :], w[:, :]).then_inc(w_in, 16)
            for rows_of, src, n in ((bk_rows, wk_b, P), (bv_rows, wv_b, P), (bo_rows, wo_b, S), (g_rows, ln_g, S), (b_rows, ln_b, S)):
                act_.dma_start(rows_of[:, :], src.rearrange("(o d) -> o d", o=1).to_broadcast([n, D])).then_inc(small_in, 16)
            act_.dma_start(rb_rows[:, :], router_b.rearrange("(o d) -> o d", o=1).to_broadcast([S, E])).then_inc(small_in, 16)
            act_.dma_start(rw[:, :], router_w[:, :]).then_inc(small_in, 16)
            act_.dma_start(b_cols[:, 0:1], wq_b.rearrange("(d o) -> d o", o=1)).then_inc(small_in, 16)
            act_.dma_start(b_cols[:, 1:2], wk_b.rearrange("(d o) -> d o", o=1)).then_inc(small_in, 16)
            act_.wait_ge(wT_done, 1)
            act_.activation(w_T[:, :, :], bank_x[:, :].rearrange("p (n d) -> p n d", n=4), ACT.Copy).then_inc(wT_kept, 1)

            def normalise_x(g):
                if is_first(g):
                    act_.wait_ge(x_stats, 1)
                else:
                    act_.wait_ge(xlnT_done, g)
                    act_.wait_ge(q_bo_ready, g)
                for j in range(GB):
                    last = act_.activation(xln[:, j, :], x_all[:, bass.ds(g * (GB * D) + j * D, D)], ACT.Identity,
                                           bias=x_nb[:, bass.ds(g * GB + j, 1)], scale=x_rstd[:, bass.ds(g * GB + j, 1)])
                last.then_inc(xln_ready, 1)

            def keep_q(g):
                act_.wait_ge(xlnT_done, g + 1)
                act_.activation(xlnT[:, :], bank_x[:, 0:GB * S], ACT.Copy).then_inc(xlnT_kept, 1)
                act_.wait_ge(q_done, g + 1)
                if is_first(g):
                    act_.wait_ge(consts_ready, 1)
                act_.activation(qT[:, :], bank_q[:, 0:GB * S], ACT.Identity, bias=bq_dk[:, 0:1], scale=1.0 / DK).then_inc(q_kept, 1)

            def keep_gram(g, pair):
                act_.wait_ge(gram_done, GB * g + 2 * pair + 2)
                act_.activation(gram[:, 2 * pair:2 * pair + 2, :],
                                bank_g[pair][:, 0:2 * CW].rearrange("p (j d) -> p j d", j=2), ACT.Copy).then_inc(gram_kept, 1)

            def column_sums(g, pair):
                act_.wait_ge(gram_kept, 2 * g + pair + 1)
                if is_first(g):
                    act_.wait_ge(small_in, 16 * 9)
                else:
                    act_.wait_ge(u_kept, g)
                for j in (2 * pair, 2 * pair + 1):
                    last = act_.activation(s_bk[:, j, :], bk_rows[:, :], ACT.Identity, scale=gram[:, j, D:CW])
                last.then_inc(s_bk_ready, 1)

            def keep_c(h):
                act_.wait_ge(c_done, h + 1)
                act_.activation(ctxT[:, :], bank_c[:, 0:GB * S], ACT.Copy).then_inc(c_kept, 1)

            def keep_hT(h):
                act_.wait_ge(hT_done, h + 1)
                act_.activation(hT[:, :], bank_q[:, 0:GB * S], ACT.Copy).then_inc(hT_kept, 1)

            def root(h, n):
                act_.wait_ge(var_ready, 2 * h + n + 1)
                act_.activation(std[:, 0:GB], ve[:, 0:GB], ACT.Sqrt).then_inc(std_ready, 1)

            act_.wait_ge(x_var_ready, 1)
            act_.activation(std[:, :], ve[:, :], ACT.Sqrt).then_inc(x_std_ready, 1)
            normalise_x(0)
            keep_gram(0, 0)
            column_sums(0, 0)
            keep_q(0)
            keep_gram(0, 1)
            column_sums(0, 1)

            def round_of(g):
                normalise_x(g)
                if not isinstance(g, int) or g > 1:
                    keep_hT(g - 2)
                keep_c(g - 1)
                keep_gram(g, 0)
                column_sums(g, 0)
                keep_q(g)
                root(g - 1, 0)
                keep_gram(g, 1)
                column_sums(g, 1)
                root(g - 1, 1)

            round_of(1)
            round_of(2)
            with act_.Fori(3, NG) as g:
                round_of(g)
            keep_hT(NG - 2)
            keep_c(NG - 1)
            root(NG - 1, 0)
            root(NG - 1, 1)
            keep_hT(NG - 1)
            act_.wait_ge(below_ready, NG)
            act_.activation(th[:, :, :], below[:, :, :], ACT.Tanh, scale=0.5).then_inc(th_ready, 1)

            def keep_h2T(t, slot):
                act_.wait_ge(h2T_done, t + 1)
                if not (isinstance(t, int) and t < 2):
                    act_.wait_ge(g_done, t - 1)
                act_.activation(h2T[:, slot, :], bank_x[:, 0:P], ACT.Copy).then_inc(h2T_kept, 1)

            def silu(t, slot):
                act_.wait_ge(a_done, t + 1)
                if not (isinstance(t, int) and t < 2):
                    act_.wait_ge(act_ready, t - 1)
                act_.activation(gate_s[:, slot, :], bank_g[0][:, :], ACT.Silu).then_inc(silu_done, 1)

            keep_h2T(0, 0)
            silu(0, 0)
            keep_h2T(1, 1)
            silu(1, 1)
            keep_h2T(2, 0)
            with act_.Fori(1, TILES // 2 - 1) as i:
                silu(2 * i, 0)
                keep_h2T(2 * i + 1, 1)
                silu(2 * i + 1, 1)
                keep_h2T(2 * i + 2, 0)
            silu(TILES - 2, 0)
            keep_h2T(TILES - 1, 1)
            silu(TILES - 1, 1)

        @block.vector
        def _(v):
            step = Steps(v, dve)

            def rsqrt(n, final, deviations, meanwhile=None):
                step.done(v.tensor_scalar(half[:, 0:n], ve[:, 0:n], -0.5, None, ALU.mult))
                if meanwhile:
                    meanwhile()
                if not is_first(deviations):
                    v.wait_ge(std_ready, deviations)
                step.done(v.reciprocal(y0[:, 0:n], std[:, 0:n]))
                step.then()
                step.done(v.tensor_tensor(sq[:, 0:n], y0[:, 0:n], y0[:, 0:n], ALU.mult))
                step.then()
                step.done(v.tensor_tensor(sq[:, 0:n], sq[:, 0:n], half[:, 0:n], ALU.mult))
                step.then()
                step.done(v.scalar_tensor_tensor(out=final, in0=sq[:, 0:n], scalar=1.5, in1=y0[:, 0:n],
                                                 op0=ALU.add, op1=ALU.mult))
                step.then()

            for e in range(E):
                step.done(v.memset(first_w[:, :, e], float(E - e)))
            v.wait_ge(x_in, 16)
            for b in range(B):
                step.done(v.bn_stats(stats[:, b, :], x_all[:, b * D:(b + 1) * D]))
            step.then()
            for b in range(B):
                step.done(v.bn_aggr(mv[:, b, :], stats[:, b, :]))
            step.then()
            v.tensor_scalar(ve[:, :], mv[:, :, 1], LN_EPS, None, ALU.add).then_inc(x_var_ready, 1)
            v.wait_ge(x_var_ready, 1)
            v.wait_ge(x_std_ready, 1)
            rsqrt(B, x_rstd[:, :], 0)
            v.scalar_tensor_tensor(out=x_nb[:, :], in0=mv[:, :, 0], scalar=-1.0, in1=x_rstd[:, :],
                                   op0=ALU.mult, op1=ALU.mult).then_inc(x_stats, 1)
            v.wait_ge(small_in, 16 * 9)
            v.wait_ge(pool_set, 17)
            step.done(v.tensor_scalar(bq_dk[:, :], b_cols[:, 0:1], 1.0 / DK, None, ALU.mult))
            step.done(v.tensor_scalar(bk_s2[:, :], b_cols[:, 1:2], float(S2), None, ALU.mult))
            step.done(v.tensor_copy(region[:, :], next_i[:, :]))
            step.done(v.tensor_copy(next_free[:, :], next_i[:, :]))
            step.done(v.tensor_copy(stair[:, :], stair_i[:, :]))
            step.done(v.tensor_copy(tile_no[:, :], tile_i[:, :]))
            step.done(v.tensor_copy(e_no[:, :], e_i[:, :]))
            v.tensor_tensor(bv_mask[:, :], bv_rows[:, :], head_mask[:, :], ALU.mult).then_inc(consts_ready, 1)
            step.then()
            setup_steps = step.count

            def per_row(a):
                return a.unsqueeze(2).to_broadcast([S, GB, E])

            def layer_norm_stats(src, final, h, n, between, meanwhile=None):
                for j in range(GB):
                    step.done(v.bn_stats(stats[:, j, :], src[:, j, 0:D]))
                step.then()
                step.done(between())
                for j in range(GB):
                    step.done(v.bn_aggr(mv[:, j, :], stats[:, j, :]))
                step.then()
                v.tensor_scalar(ve[:, 0:GB], mv[:, 0:GB, 1], LN_EPS, None, ALU.add).then_inc(var_ready, 1)
                v.wait_ge(var_ready, 2 * h + n + 1)
                rsqrt(GB, final, 2 * h + n + 1, meanwhile)

            def group(tile, h):
                return tile[:, bass.ds(h * GB, GB)]

            def choose(h):
                v.wait_ge(logit_done, h + 1)
                step.done(v.tensor_tensor(logit[:, :, :], ps_logit.rearrange("p (j e) -> p j e", j=GB),
                                          rb_rows[:, :].unsqueeze(1).to_broadcast([S, GB, E]), ALU.add))
                step.then()
                step.done(v.tensor_reduce(best[:, :], logit[:, :, :], AX, ALU.max))
                step.then()
                v.tensor_tensor(group(below, h), logit[:, :, :], per_row(best[:, :]), ALU.subtract).then_inc(below_ready, 1)
                v.wait_ge(below_ready, h + 1)
                step.done(v.scalar_tensor_tensor(out=score[:, :, :], in0=group(below, h), scalar=0.0, in1=first_w[:, :, :],
                                                 op0=ALU.is_ge, op1=ALU.mult))
                step.then()
                step.done(v.tensor_reduce(best[:, :], score[:, :, :], AX, ALU.max))
                step.then()
                v.tensor_tensor(choice[:, :, :], score[:, :, :], per_row(best[:, :]), ALU.is_equal).then_inc(choice_ready, 1)

            def place(h):
                v.wait_ge(rank_done, h + 1)
                step.done(v.tensor_tensor(rank[:, :, :], ps_rank.rearrange("p (j e) -> p j e", j=GB),
                                          next_free[0:S, :].unsqueeze(1).to_broadcast([S, GB, E]), ALU.add))
                step.then()
                step.done(v.tensor_tensor(rank[:, :, :], rank[:, :, :], choice[:, :, :], ALU.mult))
                v.tensor_tensor(next_free[:, :], next_free[:, :], ps_count, ALU.add).then_inc(rank_kept, 1)
                step.then()
                step.done(v.tensor_reduce(pos[:, :], rank[:, :, :], AX, ALU.add))
                if not is_first(h):
                    v.wait_ge(map_out, 16 * GB * h)
                step.done(v.tensor_scalar(row_no[:, :], row_no[:, :], float(GB * S), None, ALU.add))
                step.then()
                step.done(v.tensor_copy(pos_i[:, :], pos[:, :]))
                step.then()
                step.done(v.tensor_single_scalar(low[:, :], pos_i[:, :], P - 1, ALU.bitwise_and))
                step.done(v.tensor_single_scalar(high[:, :], pos_i[:, :], P.bit_length() - 1, ALU.logical_shift_right))
                step.then()
                v.wait_ge(rank_kept, h + 1)
                v.scalar_tensor_tensor(out=map_i[:, :], in0=low[:, :], scalar=float(COLS), in1=high[:, :],
                                       op0=ALU.mult, op1=ALU.add).then_inc(map_i_ready, 1)

            FRONT_STEPS, BACK_STEPS = 35, 11

            def group_front(h, behind):
                v.wait_ge(mask_in, 16 * (h + 1))
                v.tensor_reduce(group(masked, h), mask_sb[:, :, :].bitcast(I32), AX, ALU.max).then_inc(mask_used, 1)
                v.wait_ge(w_done, h + 1)
                v.tensor_scalar(w4[:, :], ps_w, bk_s2[:, 0:1], None, ALU.add).then_inc(w4_ready, 1)
                v.wait_ge(u_done, h + 1)
                v.wait_ge(s_bk_ready, 2 * (h + 1))
                v.tensor_tensor(u_sb[:, :, :], bank_u[:, :].rearrange("p (j d) -> p j d", j=GB), s_bk[:, :, :],
                                ALU.add).then_inc(u_kept, 1)
                v.wait_ge(m_done, h + 1)
                step.done(v.tensor_tensor(m_own[:, :, :], bank_m[:, :].rearrange("p (j d) -> p j d", j=GB),
                                          head_mask[:, :].unsqueeze(1).to_broadcast([P, GB, D]), ALU.mult))
                v.wait_ge(w_bv_ready, h + 1)
                step.then()
                v.tensor_tensor(m_sb[:, :, :], m_own[:, :, :], w_bv[:, :, :], ALU.add).then_inc(m_kept, 1)
                if behind:
                    choose(h - 1)
                v.wait_ge(o_done, h + 1)
                v.wait_ge(q_bo_ready, h + 1)
                v.tensor_tensor(res[:, :, :], bank_u[0:S, :].rearrange("p (j d) -> p j d", j=GB), q_bo[:, :, :],
                                ALU.add).then_inc(res_ready, 1)
                v.wait_ge(res_ready, h + 1)

                def centred():
                    for j in range(GB):
                        step.done(v.scalar_tensor_tensor(out=nrm[:, j, :], in0=res[:, j, :], scalar=mv[:, j, 0:1],
                                                         in1=g_rows[:, :], op0=ALU.subtract, op1=ALU.mult))
                    if behind:
                        place(h - 1)

                layer_norm_stats(res, r_rstd[:, :], h, 0, lambda: v.memset(unused[:, :], 0.0), centred)
                v.wait_ge(x_b_ready, h + 1)
                own_rows = group(rows, h)
                for j in range(GB):
                    last = v.scalar_tensor_tensor(out=own_rows[:, j, 0:D], in0=nrm[:, j, :], scalar=r_rstd[:, j:j + 1],
                                                  in1=x_b[:, j, :], op0=ALU.mult, op1=ALU.add)
                last.then_inc(x1_ready, 1)
                v.wait_ge(x1_ready, h + 1)
                step.done(v.memset(unused[:, :], 0.0))
                layer_norm_stats(own_rows, own_rows[:, :, RSTD], h, 1, lambda: v.memset(unused[:, :], 0.0))
                step.done(v.tensor_copy(own_rows[:, :, MEAN], mv[:, 0:GB, 0]))
                for j in range(GB):
                    last = v.tensor_scalar(h_sb[:, j, :], own_rows[:, j, 0:D], mv[:, j, 0:1],
                                           own_rows[:, j, RSTD:RSTD + 1], ALU.subtract, ALU.mult)
                last.then_inc(h_ready, 1)

            step.begin(setup_steps)
            group_front(0, False)
            assert step.count == FRONT_STEPS, step.count
            step.begin(setup_steps + FRONT_STEPS)
            group_front(1, True)
            assert step.count == FRONT_STEPS + BACK_STEPS, step.count
            with v.Fori(2, NG) as h:
                step.begin(setup_steps + FRONT_STEPS * h + BACK_STEPS * (h - 1))
                group_front(h, True)
            step.begin(setup_steps + FRONT_STEPS * NG + BACK_STEPS * (NG - 1))
            choose(NG - 1)
            place(NG - 1)

            v.wait_ge(th_ready, 1)
            step.done(v.tensor_scalar(e1[:, :, :], th[:, :, :], -1.0, 1.0, ALU.mult, ALU.add))
            step.done(v.tensor_scalar(nan_or_0[:, :], masked[:, :], 0.0, NAN_BITS, ALU.is_gt, ALU.mult))
            step.then()
            step.done(v.reciprocal(e2[:, :, :], e1[:, :, :]))
            step.then()
            step.done(v.scalar_tensor_tensor(out=e3[:, :, :], in0=th[:, :, :], scalar=1.0, in1=e2[:, :, :],
                                             op0=ALU.add, op1=ALU.mult))
            step.then()
            step.done(v.tensor_reduce(esum[:, :], e3[:, :, :], AX, ALU.add))
            step.then()
            step.done(v.reciprocal(e_inv[:, :], esum[:, :]))
            step.then()
            v.tensor_tensor(rows[:, :, GATE], e_inv[:, :], nan_or_0[:, :].bitcast(F32), ALU.add).then_inc(rows_ready, 1)


            def over_t(a):
                return a.unsqueeze(1).to_broadcast([P, TILES, E])

            def over_e(a):
                return a.unsqueeze(2).to_broadcast([P, TILES, E])

            step.done(v.tensor_tensor(count[:, :], next_free[:, :], region[:, :], ALU.subtract))
            step.then()
            step.done(v.tensor_tensor(more[:, :, :], count[:, :].unsqueeze(2).to_broadcast([P, E, NT_MAX]),
                                      stair[:, :].unsqueeze(1).to_broadcast([P, E, NT_MAX]), ALU.is_gt))
            step.then()
            step.done(v.tensor_reduce(nt[:, :], more[:, :, :], AX, ALU.add))
            step.then()
            step.done(v.tensor_tensor(nt_all[:, :, :], nt[:, :].unsqueeze(1).to_broadcast([P, E, E]), upto[:, :, :],
                                      ALU.mult))
            step.then()
            step.done(v.tensor_reduce(end[:, :], nt_all[:, :, :], AX, ALU.add))
            step.then()
            step.done(v.tensor_tensor(first[:, :], end[:, :], nt[:, :], ALU.subtract))
            step.done(v.tensor_tensor(own_b[:, :, :], over_e(tile_no[:, :]), over_t(end[:, :]), ALU.is_lt))
            step.then()
            step.done(v.tensor_tensor(own_a[:, :, :], over_e(tile_no[:, :]), over_t(first[:, :]), ALU.is_ge))
            step.done(v.scalar_tensor_tensor(out=from_e[:, :], in0=region[:, :], scalar=1.0 / P, in1=first[:, :],
                                             op0=ALU.mult, op1=ALU.subtract))
            step.then()
            step.done(v.tensor_tensor(own[:, :, :], own_a[:, :, :], own_b[:, :, :], ALU.mult))
            step.done(v.scalar_tensor_tensor(out=col_te[:, :, :], in0=over_e(tile_no[:, :]), scalar=-float(COLS),
                                             in1=over_t(from_e[:, :]), op0=ALU.add, op1=ALU.add))
            step.then()
            step.done(v.tensor_tensor(pick[:, 0, :, :], own[:, :, :], over_t(e_no[:, :]), ALU.mult))
            step.done(v.tensor_tensor(pick[:, 1, :, :], own[:, :, :], col_te[:, :, :], ALU.mult))
            step.then()
            step.done(v.tensor_reduce(picked[:, :, :], pick[:, :, :, :], AX, ALU.add))
            step.then()
            v.tensor_copy(expert_i[:, :], picked[:, 0, :])
            v.tensor_scalar(col_i[:, :], picked[:, 1, :], float(COLS), None, ALU.add).then_inc(table_ready, 1)

            def at(t, column, n):
                return slots[:, bass.ds(t * ROW + column, n)]

            def normalise(t, slot, i):
                v.wait_ge(gathered[slot], 16 * (i + 1))
                if not (isinstance(t, int) and t < 2):
                    v.wait_ge(h2T_done, t - 1)
                v.tensor_scalar(h2[:, slot, :], at(t, 0, D), at(t, MEAN, 1), at(t, RSTD, 1),
                                ALU.subtract, ALU.mult).then_inc(h2_ready, 1)

            def keep_actT(t, slot):
                v.wait_ge(actT_done, t + 1)
                v.tensor_copy(actT[:, slot, :], bank_c[:, :]).then_inc(actT_kept, 1)

            def product(t, slot):
                v.wait_ge(silu_done, t + 1)
                v.wait_ge(g_done, t + 1)
                v.tensor_tensor(act[:, slot, :], gate_s[:, slot, :], bank_g[1][:, :], ALU.mult).then_inc(act_ready, 1)

            def finish(t, slot, i):
                v.wait_ge(y_done, t + 1)
                if not (isinstance(t, int) and t < 2):
                    v.wait_ge(out_written[slot], 16 * i)
                v.scalar_tensor_tensor(out=out_sb[:, slot, :], in0=bank_u[:, 0:D], scalar=at(t, GATE, 1), in1=at(t, 0, D),
                                       op0=ALU.mult, op1=ALU.add).then_inc(out_ready, 1)

            normalise(0, 0, 0)
            normalise(1, 1, 0)
            product(0, 0)
            normalise(2, 0, 1)
            keep_actT(0, 0)
            product(1, 1)
            finish(0, 0, 0)
            normalise(3, 1, 1)

            def two_tiles(i):
                for k in range(2):
                    t = 2 * i + k
                    keep_actT(t - 1, 1 - k)
                    product(t, k)
                    finish(t - 1, 1 - k, i - 1 + k)
                    normalise(t + 2, k, i + 1)

            two_tiles(1)
            with v.Fori(2, TILES // 2 - 1) as i:
                two_tiles(i)
            for t in (TILES - 2, TILES - 1):
                keep_actT(t - 1, (t - 1) % 2)
                product(t, t % 2)
                finish(t - 1, (t - 1) % 2, (t - 1) // 2)
            keep_actT(TILES - 1, 1)
            finish(TILES - 1, 1, (TILES - 1) // 2)

        @block.tensor
        def _(pe):
            pe.wait_ge(w_in, 64)
            pe.wait_ge(ident_set, 1)
            for n in range(4):
                last = pe.transpose(bank_x[:, n * D:(n + 1) * D], w_raw[:, n, :], ident[:, :])
            last.then_inc(wT_done, 1)
            wkT, wvT, wqT, woT = w_T[:, 1, :], w_T[:, 2, :], w_T[:, 0, :], w_T[:, 3, :]

            def gram_of(g, j, between=()):
                between = dict(between)
                pe.wait_ge(ctx_in[j], 32 * (g + 1))
                if not is_first(g) and j % 2 == 0:
                    pe.wait_ge(gram_kept, 2 * (g - 1) + j // 2 + 1)
                to = bank_g[j // 2][:, (j % 2) * CW:(j % 2 + 1) * CW]
                for c in range(NCH):
                    last = pe.matmul(to, ctx_sb[:, j, c, 0:D], ctx_sb[:, j, c, :], start=(c == 0), stop=(c == NCH - 1))
                    if c in between:
                        for stage, of in between[c]:
                            stage(of)
                last.then_inc(gram_done, 1)

            def u_of(h):
                pe.wait_ge(gram_kept, 2 * (h + 1))
                if is_first(h):
                    pe.wait_ge(wT_kept, 1)
                else:
                    pe.wait_ge(res_ready, h)
                for j in range(GB):
                    last = pe.matmul(bank_u[:, j * D:(j + 1) * D], gram[:, j, 0:D], wkT, start=True, stop=True)
                last.then_inc(u_done, 1)

            def w_of(h):
                pe.matmul(ps_w, wkT, gram[:, :, D], start=True, stop=True).then_inc(w_done, 1)

            def m_of(h):
                pe.wait_ge(u_kept, h + 1)
                for j in range(GB):
                    last = pe.matmul(bank_m[:, j * D:(j + 1) * D], u_sb[:, j, :], wvT, start=True, stop=True)
                last.then_inc(m_done, 1)

            def c_of(h):
                pe.wait_ge(m_kept, h + 1)
                pe.wait_ge(q_kept, h + 1)
                for j in range(GB):
                    last = pe.matmul(bank_c[:, j * S:(j + 1) * S], m_sb[:, j, :], qT[:, j * S:(j + 1) * S],
                                     start=True, stop=True)
                last.then_inc(c_done, 1)

            def o_of(h):
                pe.wait_ge(c_kept, h + 1)
                for j in range(GB):
                    last = pe.matmul(bank_u[0:S, j * D:(j + 1) * D], ctxT[:, j * S:(j + 1) * S], woT,
                                     start=True, stop=True)
                last.then_inc(o_done, 1)

            def xT_of(g):
                pe.wait_ge(xln_ready, g + 1)
                if is_first(g):
                    pe.wait_ge(wT_kept, 1)
                else:
                    pe.wait_ge(xlnT_kept, g)
                for j in range(GB):
                    last = pe.transpose(bank_x[:, j * S:(j + 1) * S], xln[:, j, :], ident[0:S, 0:S])
                last.then_inc(xlnT_done, 1)

            def q_of(g):
                pe.wait_ge(xlnT_kept, g + 1)
                if not isinstance(g, int) or g > 1:
                    pe.wait_ge(hT_kept, g - 1)
                pe.matmul(bank_q[:, 0:GB * S], wqT, xlnT[:, :], start=True, stop=True).then_inc(q_done, 1)

            def hT_of(h):
                pe.wait_ge(h_ready, h + 1)
                pe.wait_ge(q_kept, h + 2 if not isinstance(h, int) or h < NG - 1 else NG)
                for j in range(GB):
                    last = pe.transpose(bank_q[:, j * S:(j + 1) * S], h_sb[:, j, :], ident[0:S, 0:S])
                last.then_inc(hT_done, 1)

            def logits_of(h):
                pe.wait_ge(hT_kept, h + 1)
                if is_first(h):
                    pe.wait_ge(small_in, 16 * 9)
                for j in range(GB):
                    last = pe.matmul(ps_logit[:, j * E:(j + 1) * E], hT[:, j * S:(j + 1) * S], rw[:, :],
                                     start=True, stop=True)
                last.then_inc(logit_done, 1)

            def ranks_of(h):
                pe.wait_ge(choice_ready, h + 1)
                if is_first(h):
                    pe.wait_ge(pool_set, 9)
                pe.matmul(ps_rank, before[:, :], choice[:, :, :].rearrange("q j e -> q (j e)"), start=True, stop=False)
                for j in range(GB - 1):
                    n = GB - 1 - j
                    pe.matmul(ps_rank[:, (j + 1) * E:].rearrange("q (n e) -> q n e", n=n), ones[:, 0:S],
                              choice[:, j:j + 1, :].to_broadcast([S, n, E]), start=False, stop=(n == 1))
                for j in range(GB):
                    last = pe.matmul(ps_count, ones[:, :], choice[:, j, :], start=(j == 0), stop=(j == GB - 1))
                last.then_inc(rank_done, 1)

            gram_of(0, 0)
            gram_of(0, 1)
            xT_of(0)
            gram_of(0, 2, {NCH // 2: [(q_of, 0)]})
            gram_of(0, 3)

            def round_of(g):
                behind = not isinstance(g, int) or g > 1
                gram_of(g, 0, {1: [(u_of, g - 1), (w_of, g - 1)],
                               9: [(hT_of, g - 2)] if behind else []})
                gram_of(g, 1, {0: [(m_of, g - 1)],
                               2: [(logits_of, g - 2)] if behind else [],
                               7: [(c_of, g - 1)],
                               11: [(o_of, g - 1)]})
                gram_of(g, 2, {4: [(ranks_of, g - 2)] if behind else [],
                               7: [(xT_of, g)],
                               11: [(q_of, g)]})
                gram_of(g, 3)

            round_of(1)
            round_of(2)
            with pe.Fori(3, NG) as g:
                round_of(g)
            for stage, h in ((u_of, NG - 1), (w_of, NG - 1), (hT_of, NG - 2), (m_of, NG - 1), (logits_of, NG - 2),
                             (c_of, NG - 1), (o_of, NG - 1), (ranks_of, NG - 2), (hT_of, NG - 1),
                             (logits_of, NG - 1), (ranks_of, NG - 1)):
                stage(h)

            def h2T_of(t, slot):
                pe.wait_ge(h2_ready, t + 1)
                if not is_first(t):
                    pe.wait_ge(h2T_kept, t)
                pe.transpose(bank_x[:, 0:P], h2[:, slot, :], ident[:, :]).then_inc(h2T_done, 1)

            def up(t, slot, part_, expert):
                if part_ == 0:
                    pe.wait_ge(h2T_kept, t + 1)
                if not is_first(t):
                    pe.wait_ge(*((silu_done, t) if part_ == 0 else (act_ready, t)))
                pe.matmul(bank_g[part_][:, :], h2T[:, slot, :], w1_sb[:, bass.ds(expert * F2 + part_ * FF, FF)],
                          start=True, stop=True).then_inc((a_done, g_done)[part_], 1)

            def actT_of(t, slot):
                pe.wait_ge(act_ready, t + 1)
                if not is_first(t):
                    pe.wait_ge(actT_kept, t)
                for c in range(FC):
                    last = pe.transpose(bank_c[:, c * P:(c + 1) * P], act[:, slot, c * P:(c + 1) * P], ident[:, :])
                last.then_inc(actT_done, 1)

            def down(t, slot, expert):
                pe.wait_ge(actT_kept, t + 1)
                if not is_first(t):
                    pe.wait_ge(out_ready, t)
                for c in range(FC):
                    last = pe.matmul(bank_u[:, 0:D], actT[:, slot, c * P:(c + 1) * P],
                                     w2_sb[:, bass.ds(expert * (FC * D) + c * D, D)], start=(c == 0), stop=(c == FC - 1))
                last.then_inc(y_done, 1)

            def expert_of(t):
                return pe.value_load(expert_i[0:1, bass.ds(t, 1)], min_val=0, max_val=E - 1)

            pe.wait_ge(table_ready, 1)
            pe.wait_ge(w1_in, 16 * E)
            pe.wait_ge(w2_in, 16 * E)
            h2T_of(0, 0)
            here = expert_of(0)
            up(0, 0, 0, here)
            h2T_of(1, 1)
            up(0, 0, 1, here)

            def tile(t, slot):
                here = expert_of(t)
                up(t, slot, 0, here)
                if not (isinstance(t, int) and t == TILES - 1):
                    h2T_of(t + 1, 1 - slot)
                actT_of(t - 1, 1 - slot)
                up(t, slot, 1, here)
                down(t - 1, 1 - slot, expert_of(t - 1))

            tile(1, 1)
            tile(2, 0)
            with pe.Fori(1, TILES // 2 - 1) as i:
                tile(2 * i + 1, 1)
                tile(2 * i + 2, 0)
            tile(TILES - 1, 1)
            actT_of(TILES - 1, 1)
            down(TILES - 1, 1, expert_of(TILES - 1))


def kernel(**inputs):
    import concourse.bacc as bacc
    import numpy as np
    from concourse.bass_utils import run_bass_kernel_spmd

    names = ("x", "ctx_1024", "mask_Bx1xSxS2_bf0", "L0_xattn_wq_w", "L0_xattn_wq_b", "L0_xattn_wk_w", "L0_xattn_wk_b",
             "L0_xattn_wv_w", "L0_xattn_wv_b", "L0_xattn_wo_w", "L0_xattn_wo_b", "L0_xattn_ln_g", "L0_xattn_ln_b",
             "L0_ffn_router_w", "L0_ffn_router_b", "L0_ffn_w1", "L0_ffn_w2")
    nc = bacc.Bacc("TRN2", target_bir_lowering=False, num_devices=1)
    arrays, args = {}, []
    for name in names:
        a = np.ascontiguousarray(inputs[name])
        arrays[name] = a
        args.append(nc.dram_tensor(name, a.shape, mybir.dt.from_np(a.dtype), kind="ExternalInput").ap())
    out = nc.dram_tensor("out", arrays["x"].shape, F32, kind="ExternalOutput").ap()
    build(nc, *args, out)
    return run_bass_kernel_spmd(nc, [arrays], core_ids=[0]).results[0]["out"]
```

```python
from contextlib import ExitStack

import concourse.bass as bass
from concourse import mybir

ALU = mybir.AluOpType
ACT = mybir.ActivationFunctionType
AX = mybir.AxisListType.X
F32 = mybir.dt.float32
F32R = mybir.dt.float32r
BF16 = mybir.dt.bfloat16
F16 = mybir.dt.float16
I32 = mybir.dt.int32
U8 = mybir.dt.uint8

P = 128
LN_EPS = 1e-5
HEADS = 16
DK = 2.828125
NAN_BITS = 2143289344.0
SKIP = 1000000


class Steps:

    def __init__(self, engine, semaphore):
        self.engine, self.semaphore, self.base, self.count = engine, semaphore, 0, 0

    def begin(self, base):
        self.base, self.count = base, 0

    def done(self, instruction):
        instruction.then_inc(self.semaphore, 1)
        self.count += 1

    def then(self, count=None):
        self.engine.wait_ge(self.semaphore, self.base + (self.count if count is None else count))


def build(nc, x, ctx_rows, mask, wq_w, wq_b, wk_w, wk_b, wv_w, wv_b, wo_w, wo_b, ln_g, ln_b,
          router_w, router_b, w1, w2, out):
    B, S, D = x.shape
    S2 = ctx_rows.shape[1]
    E, _, F2 = w1.shape
    FF = F2 // 2
    HD = D // HEADS
    assert D == P and HD == 8 and FF % P == 0 and S2 % 4 == 0

    GB = 4
    NG = B // GB
    EP = E // NG
    FULL = S2 // P
    REST = S2 - FULL * P
    NCH = FULL + 1
    CW = D + 1
    TOKENS = B * S
    TILES = (TOKENS + E * (P - 1)) // P
    MAIN = (TOKENS + E * P // 2 + P - 1) // P
    ROW = D + 3
    MEAN, RSTD, GATE = D, D + 1, D + 2
    FC = FF // P
    MW = S2 // 4
    NT_MAX = (TOKENS + P - 1) // P
    COLS = E * NT_MAX
    FLIGHT = 4
    AHEAD = 8
    PACK = 8
    WORDS = (TILES + PACK - 1) // PACK
    PT = WORDS * PACK
    assert E <= 8
    assert COLS <= P and TOKENS < 2048

    token_rows = nc.dram_tensor("token_rows", (TOKENS, ROW), F32, kind="Internal").ap()
    out_rows = out.rearrange("b s d -> (b s) d")

    with ExitStack() as stack:
        def sb(name, shape, dtype=F32):
            return stack.enter_context(nc.sbuf_tensor(name, shape, dtype))

        def bank(name, shape):
            return stack.enter_context(nc.psum_tensor(name, shape, F32))

        def sem(name):
            return stack.enter_context(nc.semaphore(name))

        w_raw = sb("w_raw", [P, 4, D])
        w_T = sb("w_T", [P, 4, D])
        bk_rows = sb("bk_rows", [P, D])
        bv_rows = sb("bv_rows", [P, D])
        bo_rows = sb("bo_rows", [S, D])
        g_rows = sb("g_rows", [S, D])
        b_rows = sb("b_rows", [S, D])
        rb_rows = sb("rb_rows", [S, E])
        rw = sb("rw", [P, E])
        b_cols = sb("b_cols", [P, 2])
        bq_dk = sb("bq_dk", [P, 1])
        bk_s2 = sb("bk_s2", [P, 1])
        w1_sb = sb("w1_sb", [P, E * F2])
        w1_high, w1_low = sb("w1_high", [P, E * F2], F32R), sb("w1_low", [P, E * F2], F32R)
        w2_sb = sb("w2_sb", [P, E * FC * D])
        ident = sb("ident", [P, P])
        head_mask = sb("head_mask", [P, D])
        bv_mask = sb("bv_mask", [P, D])
        before = sb("before", [S, S], BF16)
        ones = sb("ones", [S, P], BF16)
        idle = sb("idle", [P, 512], BF16)
        first_w = sb("first_w", [S, GB, E])

        ctx_sb = sb("ctx_sb", [P, GB, NCH, CW])
        gram = sb("gram", [P, GB, CW])
        s_bk = sb("s_bk", [P, GB, D])
        w4 = sb("w4", [P, GB])
        w_bv = sb("w_bv", [P, GB, D])
        u_sb = sb("u_sb", [P, GB, D])
        m_sb = sb("m_sb", [P, GB, D])
        xln = sb("xln", [S, GB, D])
        xlnT = sb("xlnT", [P, GB * S])
        qT = sb("qT", [P, GB * S])
        ctxT = sb("ctxT", [P, GB * S])
        q_bo = sb("q_bo", [S, GB, D])
        x_b = sb("x_b", [S, GB, D])
        res = sb("res", [S, GB, D])
        rows = sb("rows", [S, B, ROW])
        h_sb = sb("h_sb", [S, GB, D])
        hT = sb("hT", [P, GB * S])
        stats = sb("stats", [S, B, 6])
        mv = sb("mv", [S, B, 2])
        ve = sb("ve", [S, B])
        std = sb("std", [S, B])
        half = sb("half", [S, B])
        y0 = sb("y0", [S, B])
        unused = sb("unused", [S, 1])
        one = sb("one", [S, 1])
        unused_silu = sb("unused_silu", [S, 1])
        sq = sb("sq", [S, B])
        x_rstd = sb("x_rstd", [S, B])
        x_nb = sb("x_nb", [S, B])
        h_nb = sb("h_nb", [S, GB])
        mask_sb = sb("mask_sb", [S, GB, S2], U8)
        mask_fold = sb("mask_fold", [S, GB, (MW + 1) // 2], I32)
        masked = sb("masked", [S, B])
        nan_or_0 = sb("nan_or_0", [S, B], I32)

        logit = sb("logit", [S, GB, E])
        below = sb("below", [S, B, E])
        best = sb("best", [S, GB])
        score = sb("score", [S, GB, E])
        choice = sb("choice", [S, GB, E], BF16)
        th = sb("th", [S, B, E])
        e1 = sb("e1", [S, B, E])
        e2 = sb("e2", [S, B, E])
        esum = sb("esum", [S, B])
        e_inv = sb("e_inv", [S, B])
        r_rstd = sb("r_rstd", [S, GB])
        rank = sb("rank", [S, GB, E])
        pos = sb("pos", [S, GB])
        pos_i = sb("pos_i", [S, GB], I32)
        place_i = sb("place_i", [S, 2, GB], I32)
        place_f = sb("place_f", [S, 2, GB])
        slot_hot = sb("slot_hot", [S, GB, P], F16)
        col_hot = sb("col_hot", [S, GB, COLS], F16)
        map_T = sb("map_T", [COLS, P], F16)
        slot_no_i = sb("slot_no_i", [S, P], I32)
        slot_no = sb("slot_no", [S, P], F16)
        col_no_i = sb("col_no_i", [S, COLS], I32)
        col_no = sb("col_no", [S, COLS], F16)
        number_i = sb("number_i", [S, B], I32)
        number = sb("number", [S, B])
        next_i = sb("next_i", [P, E], I32)
        next_free = sb("next_free", [P, E])

        stair_i = sb("stair_i", [P, E, NT_MAX], I32)
        stair = sb("stair", [P, E, NT_MAX])
        before_tile_i = sb("before_tile_i", [COLS, TILES], I32)
        before_tile = sb("before_tile", [COLS, TILES])
        bound_i = sb("bound_i", [P, PT, E - 1], I32)
        bound = sb("bound", [P, PT, E - 1])
        upto = sb("upto", [P, E, E])
        minus_before = sb("minus_before", [COLS, E])
        empty_cols = sb("empty_cols", [P, E, NT_MAX])
        lack = sb("lack", [P, E])
        lack_before = sb("lack_before", [COLS, E])
        shift = sb("shift", [COLS, 1])
        picks = sb("picks", [COLS, TILES], F16)
        lack_fe = sb("lack_fe", [P, E, E])
        lack_upto = sb("lack_upto", [P, E])
        past = sb("past", [P, PT, E - 1])
        digit = sb("digit", [P, WORDS, PACK, E - 1])
        experts_f = sb("experts_f", [P, WORDS])
        experts_i = sb("experts_i", [P, WORDS + 1], I32)
        skip = sb("skip", [P, TILES])

        token = sb("token", [P, TILES], I32)
        h2T_high, h2T_low = sb("h2T_high", [P, 2, P], F32R), sb("h2T_low", [P, 2, P], F32R)
        actT = sb("actT", [P, 2, FF])
        space = ctx_sb[:, :, :, :].rearrange("p j c d -> p (j c d)")
        slots = space[:, 0:TILES * ROW]
        gate_s, act = (space[:, TILES * ROW + n * FF:TILES * ROW + (n + 2) * FF].rearrange("p (s f) -> p s f", s=2)
                       for n in (0, 2))
        h2, out_sb = (space[:, TILES * ROW + 4 * FF + n * D:TILES * ROW + 4 * FF + (n + 2) * D].rearrange("p (s d) -> p s d", s=2)
                      for n in (0, 2))

        bank_g = [bank("bank_g0", [P, 512]), bank("bank_g1", [P, 512])]
        bank_c, bank_u, bank_m = bank("bank_c", [P, 512]), bank("bank_u", [P, 512]), bank("bank_m", [P, 512])
        bank_x, bank_q, bank_r = bank("bank_x", [P, 512]), bank("bank_q", [P, 512]), bank("bank_r", [P, 512])
        ps_w = bank_c[:, GB * S:GB * S + GB]
        ps_logit = bank_q[0:S, GB * S:GB * S + GB * E]
        ps_rank = bank_r[0:S, 128:128 + GB * E]
        ps_count = bank_r[:, 192:192 + E]
        ps_map = bank_r[0:COLS, 256:256 + P]
        ps_last_map = bank_g[0][0:COLS, 0:P]
        ps_token = bank_r[:, 384:384 + TILES]

        x_in, w_in, small_in = sem("x_in"), sem("w_in"), sem("small_in")
        w1_in, w2_in = sem("w1_in"), sem("w2_in")
        high_kept, low_kept = sem("high_kept"), sem("low_kept")
        ctx_in = [sem(f"ctx_in{j}") for j in range(GB)]
        mask_in = sem("mask_in")
        ones_set, idle_set = sem("ones_set"), sem("idle_set")
        pool_set = sem("pool_set")
        ident_set = sem("ident_set")
        wT_done, wT_kept = sem("wT_done"), sem("wT_kept")
        consts_ready = sem("consts_ready")
        x_var_ready, x_std_ready, x_stats = sem("x_var_ready"), sem("x_std_ready"), sem("x_stats")
        var_ready, std_ready = sem("var_ready"), sem("std_ready")
        gram_done = sem("gram_done")
        gram_kept = sem("gram_kept")
        xln_ready = sem("xln_ready")
        xlnT_done, xlnT_kept = sem("xlnT_done"), sem("xlnT_kept")
        q_done, q_kept = sem("q_done"), sem("q_kept")
        q_bo_ready, x_b_ready = sem("q_bo_ready"), sem("x_b_ready")
        s_bk_ready = sem("s_bk_ready")
        u_done, u_kept = sem("u_done"), sem("u_kept")
        w_done, w4_ready, w_bv_ready = sem("w_done"), sem("w4_ready"), sem("w_bv_ready")
        m_done, m_kept = sem("m_done"), sem("m_kept")
        c_done, c_kept = sem("c_done"), sem("c_kept")
        o_done, res_ready = sem("o_done"), sem("res_ready")
        x1_ready, h_nb_ready = sem("x1_ready"), sem("h_nb_ready")
        h_left_ready, h_right_ready = sem("h_left_ready"), sem("h_right_ready")
        hT_done, hT_kept = sem("hT_done"), sem("hT_kept")
        logit_done, below_ready, th_ready = sem("logit_done"), sem("below_ready"), sem("th_ready")
        e1_ready = sem("e1_ready")
        choice_ready, rank_done, rank_kept = sem("choice_ready"), sem("rank_done"), sem("rank_kept")
        place_ready, hot_ready = sem("place_ready"), sem("hot_ready")
        map_done, map_kept, picks_ready = sem("map_done"), sem("map_kept"), sem("picks_ready")
        rows_ready, slots_set = sem("rows_ready"), sem("slots_set")
        mask_folded, mask_reduced = sem("mask_folded"), sem("mask_reduced")
        rows_out = sem("rows_out")
        token_done = sem("token_done")
        token_ready = sem("token_ready")
        dve = sem("dve_step")
        table_ready = sem("table_ready")
        gathered = [sem(f"gathered{n}") for n in range(FLIGHT)]
        h2_ready, h2T_done = sem("h2_ready"), sem("h2T_done")
        h2T_high_kept, h2T_low_kept = sem("h2T_high_kept"), sem("h2T_low_kept")
        a_done, silu_done, g_done, act_ready = sem("a_done"), sem("silu_done"), sem("g_done"), sem("act_ready")
        actT_done, actT_kept = sem("actT_done"), sem("actT_kept")
        y_done, out_ready = sem("y_done"), sem("out_ready")
        out_written = [sem("out_written0"), sem("out_written1")]

        block = stack.enter_context(nc.Block())

        def more_tiles(engine):
            engine.wait_ge(table_ready, 1)
            main_do = engine.value_load(experts_i[0:1, WORDS:WORDS + 1], min_val=0, max_val=1)
            return engine.If(main_do < 1)

        def is_first(g):
            return isinstance(g, int) and g == 0

        def wait_alone(engine, semaphore, value, sure, sure_value):
            value = value if isinstance(value, int) else engine.snap(value)
            engine.wait_ge(sure, sure_value)
            engine.wait_ge(semaphore, value)

        def load_group(sp, g):
            for j in range(GB):
                b = g * GB + j
                row = ctx_rows[bass.ds(b, 1)].rearrange("o s d -> (o s) d")
                if is_first(g):
                    sp.wait_ge(ones_set, 1)
                else:
                    wait_alone(sp, gram_done, GB * (g - 1) + j + 1, ones_set, 1)
                sp.dma_start(ctx_sb[:, j, 0:FULL, 0:D],
                             row[0:FULL * P, :].rearrange("(p c) d -> p c d", p=P)).then_inc(ctx_in[j], 16)
                sp.dma_start(ctx_sb[0:REST, j, FULL, 0:D], row[FULL * P:S2, :]).then_inc(ctx_in[j], 16)
                if is_first(g) and j == 1:
                    sp.dma_start(rows[:, :, 0:D], x.rearrange("b q d -> q b d")).then_inc(x_in, 16)
            if not is_first(g):
                wait_alone(sp, mask_folded, g, ones_set, 1)
            sp.dma_start(mask_sb[:, :, :], mask[bass.ds(g * GB, GB), 0].rearrange("b q k -> q b k")).then_inc(mask_in, 16)

        @block.sync
        def _(sp):
            load_group(sp, 0)

            def load_experts(k):
                if not is_first(k):
                    wait_alone(sp, w1_in, 16 * k, ones_set, 1)
                    wait_alone(sp, w2_in, 16 * k, ones_set, 1)
                sp.dma_start(w1_sb[:, bass.ds(k * (EP * F2), EP * F2)].rearrange("p (e f) -> p e f", e=EP),
                             w1[bass.ds(k * EP, EP)].rearrange("e p f -> p e f")).then_inc(w1_in, 16)
                sp.dma_start(w2_sb[:, bass.ds(k * (EP * FC * D), EP * FC * D)].rearrange("p (c d) -> p c d", d=D),
                             w2[bass.ds(k * EP, EP)].rearrange("e (c p) d -> p (e c) d", p=P)).then_inc(w2_in, 16)

            load_group(sp, 1)
            load_experts(0)
            with sp.Fori(2, NG) as g:
                load_group(sp, g)
                load_experts(g - 1)
            load_experts(NG - 1)
            sp.wait_ge(rows_ready, 1)
            sp.dma_start(token_rows.rearrange("(b q) n -> q b n", b=B), rows[:, :, :]).then_inc(rows_out, 16)

        @block.gpsimd
        def _(pool):
            pool.memset(ctx_sb[:, :, FULL, :], 0.0).then_inc(pool_set, 1)
            pool.memset(ident[:, :], 0.0).then_inc(pool_set, 1)
            pool.wait_ge(pool_set, 2)
            pool.memset(ctx_sb[:, :, :, D:CW], 1.0).then_inc(ones_set, 1)
            pool.affine_select(out=ident[:, :], in_=ident[:, :], compare_op=ALU.not_equal, fill=1.0,
                               base=0, pattern=[[-1, P]], channel_multiplier=1).then_inc(ident_set, 1)
            pool.memset(head_mask[:, :], 1.0).then_inc(pool_set, 1)
            pool.memset(before[:, :], 1.0).then_inc(pool_set, 1)
            pool.memset(ones[:, :], 1.0).then_inc(pool_set, 1)
            pool.memset(upto[:, :, :], 1.0).then_inc(pool_set, 1)
            pool.wait_ge(pool_set, 6)
            heads = head_mask[:, :].rearrange("p (h d) -> p h d", d=HD)
            pool.affine_select(out=heads, in_=heads, compare_op=ALU.is_ge, fill=0.0, base=0,
                               pattern=[[-HD, HEADS], [0, HD]], channel_multiplier=1).then_inc(pool_set, 1)
            pool.affine_select(out=before[:, :], in_=before[:, :], compare_op=ALU.is_gt, fill=0.0, base=0,
                               pattern=[[1, S]], channel_multiplier=-1).then_inc(pool_set, 1)
            pool.affine_select(out=upto[:, :, :], in_=upto[:, :, :], compare_op=ALU.is_ge, fill=0.0, base=0,
                               pattern=[[1, E], [-1, E]], channel_multiplier=0).then_inc(pool_set, 1)
            pool.wait_ge(pool_set, 9)
            pool.affine_select(out=heads, in_=heads, compare_op=ALU.is_ge, fill=0.0, base=HD - 1,
                               pattern=[[HD, HEADS], [0, HD]], channel_multiplier=-1).then_inc(pool_set, 1)
            pool.memset(minus_before[:, :], -1.0).then_inc(pool_set, 1)
            pool.iota(number_i[:, :], pattern=[[S, B]], base=1, channel_multiplier=1).then_inc(pool_set, 1)
            pool.iota(next_i[:, :], pattern=[[NT_MAX * P, E]], base=0, channel_multiplier=0).then_inc(pool_set, 1)
            pool.iota(stair_i[:, :, :], pattern=[[NT_MAX * P, E], [P, NT_MAX]], base=0, channel_multiplier=0).then_inc(pool_set, 1)
            pool.iota(slot_no_i[:, :], pattern=[[1, P]], base=0, channel_multiplier=0).then_inc(pool_set, 1)
            pool.iota(col_no_i[:, :], pattern=[[1, COLS]], base=0, channel_multiplier=0).then_inc(pool_set, 1)
            pool.iota(before_tile_i[:, :], pattern=[[1, TILES]], base=0, channel_multiplier=-1).then_inc(pool_set, 1)
            pool.iota(bound_i[:, :, :], pattern=[[-1, PT], [NT_MAX, E - 1]], base=NT_MAX, channel_multiplier=0).then_inc(pool_set, 1)
            pool.wait_ge(pool_set, 18)
            pool.affine_select(out=minus_before[:, :], in_=minus_before[:, :], compare_op=ALU.is_ge, fill=0.0,
                               base=-NT_MAX, pattern=[[-NT_MAX, E]], channel_multiplier=1).then_inc(pool_set, 1)
            last_token = pool.to_reg(TOKENS - 1)

            def prepare(g):
                pool.wait_ge(xln_ready, g + 1)
                if not is_first(g):
                    pool.wait_ge(x1_ready, g)
                else:
                    pool.wait_ge(small_in, 16 * 9)
                pool.tensor_tensor(q_bo[:, :, :], xln[:, :, :],
                                   bo_rows[:, :].unsqueeze(1).to_broadcast([S, GB, D]), ALU.add).then_inc(q_bo_ready, 1)
                pool.tensor_tensor(x_b[:, :, :],
                                   rows[:, bass.ds(g * GB, GB), 0:D],
                                   b_rows[:, :].unsqueeze(1).to_broadcast([S, GB, D]), ALU.add).then_inc(x_b_ready, 1)

            def outer(h):
                if not is_first(h):
                    pool.wait_ge(m_kept, h)
                else:
                    pool.wait_ge(consts_ready, 1)
                pool.wait_ge(w4_ready, h + 1)
                pool.tensor_tensor(w_bv[:, :, :], bv_mask[:, :].unsqueeze(1).to_broadcast([P, GB, D]),
                                   w4[:, :].unsqueeze(2).to_broadcast([P, GB, D]), ALU.mult).then_inc(w_bv_ready, 1)

            def fold_mask(h):
                pool.wait_ge(mask_in, 16 * (h + 1))
                if not is_first(h):
                    pool.wait_ge(mask_reduced, h)
                words = mask_sb[:, :, :].bitcast(I32)
                pool.tensor_tensor(mask_fold[:, :, :], words[:, :, 0:(MW + 1) // 2], words[:, :, MW // 2:MW],
                                   ALU.add).then_inc(mask_folded, 1)

            def keep_low(k):
                pool.wait_ge(high_kept, k + 1)
                own = bass.ds(k * (EP * F2), EP * F2)
                pool.tensor_tensor(w1_low[:, own], w1_sb[:, own], w1_high.bitcast(F32)[:, own],
                                   ALU.subtract).then_inc(low_kept, 1)

            outer(0)
            prepare(0)
            fold_mask(0)
            fold_mask(1)
            prepare(1)
            with pool.Fori(2, NG) as g:
                outer(g - 1)
                fold_mask(g)
                keep_low(g - 2)
                prepare(g)
            outer(NG - 1)
            keep_low(NG - 2)
            pool.wait_ge(gram_done, GB * NG)
            pool.memset(slots[:, :], 0.0).then_inc(slots_set, 1)
            keep_low(NG - 1)
            pool.wait_ge(slots_set, 1)

            def gather(t):
                if t >= FLIGHT:
                    pool.wait_ge(gathered[t % FLIGHT], 16 * (t // FLIGHT))
                pool.indirect_dma_start(out=slots[:, t * ROW:(t + 1) * ROW], out_offset=None, in_=token_rows[:, :],
                                        in_offset=bass.IndirectOffsetOnAxis(ap=token[:, t:t + 1], axis=0),
                                        bounds_check=last_token, oob_is_err=False).then_inc(gathered[t % FLIGHT], 16)

            def scatter(t):
                pool.wait_ge(out_ready, t + 1)
                pool.indirect_dma_start(out=out_rows[:, :], out_offset=bass.IndirectOffsetOnAxis(ap=token[:, t:t + 1], axis=0),
                                        in_=out_sb[:, t % 2, :], in_offset=None, bounds_check=last_token,
                                        oob_is_err=False).then_inc(out_written[t % 2], 16)

            def gathers_and_scatters(start, stop):
                for t in range(start, min(start + AHEAD, stop)):
                    gather(t)
                for t in range(start, stop):
                    if t + AHEAD < stop:
                        gather(t + AHEAD)
                    scatter(t)
                pool.wait_ge(out_written[0], 16 * ((stop + 1) // 2))
                pool.wait_ge(out_written[1], 16 * (stop // 2))

            pool.wait_ge(rows_out, 16)
            pool.wait_ge(token_ready, 1)
            gathers_and_scatters(0, MAIN)
            with more_tiles(pool):
                gathers_and_scatters(MAIN, TILES)

        @block.scalar
        def _(act_):
            for n, w in enumerate((wq_w, wk_w, wv_w, wo_w)):
                act_.dma_start(w_raw[:, n, :], w[:, :]).then_inc(w_in, 16)
            for rows_of, src, n in ((bk_rows, wk_b, P), (bv_rows, wv_b, P), (bo_rows, wo_b, S), (g_rows, ln_g, S), (b_rows, ln_b, S)):
                act_.dma_start(rows_of[:, :], src.rearrange("(o d) -> o d", o=1).to_broadcast([n, D])).then_inc(small_in, 16)
            act_.dma_start(rb_rows[:, :], router_b.rearrange("(o d) -> o d", o=1).to_broadcast([S, E])).then_inc(small_in, 16)
            act_.dma_start(rw[:, :], router_w[:, :]).then_inc(small_in, 16)
            act_.dma_start(b_cols[:, 0:1], wq_b.rearrange("(d o) -> d o", o=1)).then_inc(small_in, 16)
            act_.dma_start(b_cols[:, 1:2], wk_b.rearrange("(d o) -> d o", o=1)).then_inc(small_in, 16)
            act_.wait_ge(x_var_ready, 1)
            act_.activation(std[:, :], ve[:, :], ACT.Sqrt).then_inc(x_std_ready, 1)
            act_.wait_ge(wT_done, 1)
            act_.activation(w_T[:, :, :], bank_x[:, :].rearrange("p (n d) -> p n d", n=4), ACT.Copy).then_inc(wT_kept, 1)

            def normalise_x(g):
                if is_first(g):
                    act_.wait_ge(x_stats, 1)
                else:
                    act_.wait_ge(xlnT_done, g)
                    act_.wait_ge(q_bo_ready, g)
                for j in range(GB):
                    last = act_.activation(xln[:, j, :], rows[:, bass.ds(g * GB + j, 1), 0:D].rearrange("q o d -> q (o d)"), ACT.Identity,
                                           bias=x_nb[:, bass.ds(g * GB + j, 1)], scale=x_rstd[:, bass.ds(g * GB + j, 1)])
                last.then_inc(xln_ready, 1)

            def keep_q(g):
                act_.wait_ge(xlnT_done, g + 1)
                act_.activation(xlnT[:, :], bank_x[:, 0:GB * S], ACT.Copy).then_inc(xlnT_kept, 1)
                act_.wait_ge(q_done, g + 1)
                if is_first(g):
                    act_.wait_ge(consts_ready, 1)
                act_.activation(qT[:, :], bank_q[:, 0:GB * S], ACT.Identity, bias=bq_dk[:, 0:1], scale=1.0 / DK).then_inc(q_kept, 1)

            def keep_gram(g, pair):
                act_.wait_ge(gram_done, GB * g + 2 * pair + 2)
                act_.activation(gram[:, 2 * pair:2 * pair + 2, :],
                                bank_g[pair][:, 0:2 * CW].rearrange("p (j d) -> p j d", j=2), ACT.Copy).then_inc(gram_kept, 1)

            def column_sums(g, pair):
                act_.wait_ge(gram_kept, 2 * g + pair + 1)
                if is_first(g):
                    act_.wait_ge(small_in, 16 * 9)
                else:
                    act_.wait_ge(u_kept, g)
                for j in (2 * pair, 2 * pair + 1):
                    last = act_.activation(s_bk[:, j, :], bk_rows[:, :], ACT.Identity, scale=gram[:, j, D:CW])
                last.then_inc(s_bk_ready, 1)

            def keep_c(h):
                act_.wait_ge(c_done, h + 1)
                act_.activation(ctxT[:, :], bank_c[:, 0:GB * S], ACT.Copy).then_inc(c_kept, 1)

            def keep_hT(h):
                act_.wait_ge(hT_done, h + 1)
                act_.activation(hT[:, :], bank_q[:, 0:GB * S], ACT.Copy).then_inc(hT_kept, 1)

            def root(h, n):
                act_.wait_ge(var_ready, 2 * h + n + 1)
                act_.activation(std[:, 0:GB], ve[:, 0:GB], ACT.Sqrt).then_inc(std_ready, 1)

            def right_half(h):
                act_.wait_ge(h_nb_ready, h + 1)
                for j in range(GB // 2, GB):
                    last = act_.activation(h_sb[:, j, :], rows[:, bass.ds(h * GB + j, 1), 0:D].rearrange("q o d -> q (o d)"),
                                           ACT.Identity, bias=h_nb[:, j:j + 1],
                                           scale=rows[:, bass.ds(h * GB + j, 1), RSTD])
                last.then_inc(h_right_ready, 1)

            keep_gram(0, 0)
            keep_gram(0, 1)
            column_sums(0, 0)
            column_sums(0, 1)
            normalise_x(0)
            keep_q(0)

            def round_high(k):
                act_.wait_ge(w1_in, 16 * (k + 1))
                for e in range(EP):
                    own = bass.ds(k * (EP * F2) + e * F2, F2)
                    last = act_.activation(w1_high[:, own], w1_sb[:, own], ACT.Copy)
                last.then_inc(high_kept, 1)

            def round_of(g):
                normalise_x(g)
                if not isinstance(g, int) or g > 1:
                    keep_hT(g - 2)
                keep_c(g - 1)
                keep_gram(g, 0)
                column_sums(g, 0)
                if not isinstance(g, int) or g > 1:
                    round_high(g - 2)
                keep_q(g)
                root(g - 1, 0)
                keep_gram(g, 1)
                column_sums(g, 1)
                root(g - 1, 1)
                right_half(g - 1)

            round_of(1)
            round_of(2)
            with act_.Fori(3, NG) as g:
                round_of(g)
            keep_hT(NG - 2)
            keep_c(NG - 1)
            round_high(NG - 2)
            root(NG - 1, 0)
            round_high(NG - 1)
            root(NG - 1, 1)
            right_half(NG - 1)
            keep_hT(NG - 1)
            act_.wait_ge(below_ready, NG)
            act_.activation(th[:, :, :], below[:, :, :], ACT.Tanh, scale=0.5).then_inc(th_ready, 1)
            act_.wait_ge(th_ready, 1)
            act_.activation(e1[:, :, :], th[:, :, :], ACT.Identity, bias=one[:, 0:1], scale=-1.0).then_inc(e1_ready, 1)
            act_.activation(unused_silu[:, :], th[:, 0, 0:1], ACT.Silu)

            def keep_h2T(t, slot):
                act_.wait_ge(h2T_done, t + 1)
                if t >= 2:
                    act_.wait_ge(g_done, t - 1)
                act_.activation(h2T_high[:, slot, :], bank_x[:, 0:P], ACT.Copy).then_inc(h2T_high_kept, 1)

            def silu(t, slot):
                act_.wait_ge(a_done, t + 1)
                if not (isinstance(t, int) and t < 2):
                    act_.wait_ge(act_ready, t - 1)
                act_.activation(gate_s[:, slot, :], bank_g[0][:, :], ACT.Silu).then_inc(silu_done, 1)

            def tiles(start, stop):
                keep_h2T(start, start % 2)
                for t in range(start, stop):
                    silu(t, t % 2)
                    if t + 1 < stop:
                        keep_h2T(t + 1, (t + 1) % 2)

            tiles(0, MAIN)
            with more_tiles(act_):
                tiles(MAIN, TILES)

        @block.vector
        def _(v):
            step = Steps(v, dve)
            v.memset(idle[:, :], 0.0).then_inc(idle_set, 1)

            def rsqrt(n, final, deviations, meanwhile=None):
                step.done(v.tensor_scalar(half[:, 0:n], ve[:, 0:n], -0.5, None, ALU.mult))
                if meanwhile:
                    meanwhile()
                if not is_first(deviations):
                    v.wait_ge(std_ready, deviations)
                step.done(v.reciprocal(y0[:, 0:n], std[:, 0:n]))
                step.then()
                step.done(v.tensor_tensor(sq[:, 0:n], y0[:, 0:n], y0[:, 0:n], ALU.mult))
                step.then()
                step.done(v.tensor_tensor(sq[:, 0:n], sq[:, 0:n], half[:, 0:n], ALU.mult))
                step.then()
                step.done(v.scalar_tensor_tensor(out=final, in0=sq[:, 0:n], scalar=1.5, in1=y0[:, 0:n],
                                                 op0=ALU.add, op1=ALU.mult))
                step.then()

            for e in range(E):
                step.done(v.memset(first_w[:, :, e], float(E - e)))
            step.done(v.memset(map_T[:, :], 0.0))
            step.done(v.memset(one[:, :], 1.0))
            for n in range(PACK):
                step.done(v.memset(digit[:, :, n, :], float(8 ** n)))
            v.wait_ge(x_in, 16)
            for b in range(B):
                step.done(v.bn_stats(stats[:, b, :], rows[:, b, 0:D]))
            step.then()
            for b in range(B):
                step.done(v.bn_aggr(mv[:, b, :], stats[:, b, :]))
            step.then()
            v.tensor_scalar(ve[:, :], mv[:, :, 1], LN_EPS, None, ALU.add).then_inc(x_var_ready, 1)
            v.wait_ge(x_var_ready, 1)
            v.wait_ge(x_std_ready, 1)
            rsqrt(B, x_rstd[:, :], 0)
            v.scalar_tensor_tensor(out=x_nb[:, :], in0=mv[:, :, 0], scalar=-1.0, in1=x_rstd[:, :],
                                   op0=ALU.mult, op1=ALU.mult).then_inc(x_stats, 1)
            v.wait_ge(small_in, 16 * 9)
            v.wait_ge(pool_set, 19)
            step.done(v.tensor_scalar(bq_dk[:, :], b_cols[:, 0:1], 1.0 / DK, None, ALU.mult))
            step.done(v.tensor_scalar(bk_s2[:, :], b_cols[:, 1:2], float(S2), None, ALU.mult))
            for number_of, counted in ((next_free, next_i), (slot_no, slot_no_i), (col_no, col_no_i), (number, number_i),
                                       (before_tile, before_tile_i)):
                step.done(v.tensor_copy(number_of[:, :], counted[:, :]))
            step.done(v.tensor_copy(stair[:, :, :], stair_i[:, :, :]))
            step.done(v.tensor_copy(bound[:, :, :], bound_i[:, :, :]))
            v.tensor_tensor(bv_mask[:, :], bv_rows[:, :], head_mask[:, :], ALU.mult).then_inc(consts_ready, 1)
            step.then()
            setup_steps = step.count

            def per_row(a):
                return a.unsqueeze(2).to_broadcast([S, GB, E])

            def layer_norm_stats(src, final, h, n, between, meanwhile=None):
                for j in range(GB):
                    step.done(v.bn_stats(stats[:, j, :], src[:, j, 0:D]))
                step.then()
                between()
                for j in range(GB):
                    step.done(v.bn_aggr(mv[:, j, :], stats[:, j, :]))
                step.then()
                v.tensor_scalar(ve[:, 0:GB], mv[:, 0:GB, 1], LN_EPS, None, ALU.add).then_inc(var_ready, 1)
                v.wait_ge(var_ready, 2 * h + n + 1)
                rsqrt(GB, final, 2 * h + n + 1, meanwhile)

            def group(tile, h):
                return tile[:, bass.ds(h * GB, GB)]

            def choose(h):
                v.wait_ge(logit_done, h + 1)
                step.done(v.tensor_tensor(logit[:, :, :], ps_logit.rearrange("p (j e) -> p j e", j=GB),
                                          rb_rows[:, :].unsqueeze(1).to_broadcast([S, GB, E]), ALU.add))
                step.then()
                step.done(v.tensor_reduce(best[:, :], logit[:, :, :], AX, ALU.max))
                step.then()
                v.tensor_tensor(group(below, h), logit[:, :, :], per_row(best[:, :]), ALU.subtract).then_inc(below_ready, 1)
                v.wait_ge(below_ready, h + 1)
                step.done(v.scalar_tensor_tensor(out=score[:, :, :], in0=group(below, h), scalar=0.0, in1=first_w[:, :, :],
                                                 op0=ALU.is_ge, op1=ALU.mult))
                step.then()
                step.done(v.tensor_reduce(best[:, :], score[:, :, :], AX, ALU.max))
                step.then()
                v.tensor_tensor(choice[:, :, :], score[:, :, :], per_row(best[:, :]), ALU.is_equal).then_inc(choice_ready, 1)

            def gates(stage):
                if stage == 0:
                    v.wait_ge(e1_ready, 1)
                    step.done(v.reciprocal(e2[:, :, :], e1[:, :, :]))
                elif stage == 1:
                    step.done(v.tensor_scalar(nan_or_0[:, :], masked[:, :], 0.0, NAN_BITS, ALU.is_gt, ALU.mult))
                elif stage == 2:
                    step.done(v.scalar_tensor_tensor(out=e1[:, :, :], in0=th[:, :, :], scalar=1.0, in1=e2[:, :, :],
                                                     op0=ALU.add, op1=ALU.mult))
                elif stage == 3:
                    step.done(v.tensor_reduce(esum[:, :], e1[:, :, :], AX, ALU.add))
                elif stage == 4:
                    step.done(v.reciprocal(e_inv[:, :], esum[:, :]))
                else:
                    v.tensor_tensor(rows[:, :, GATE], e_inv[:, :], nan_or_0[:, :].bitcast(F32), ALU.add).then_inc(rows_ready, 1)

            def empty_columns(stage):
                if stage == 0:
                    step.done(v.tensor_tensor(empty_cols[:, :, :], stair[:, :, :],
                                              next_free[:, :].unsqueeze(2).to_broadcast([P, E, NT_MAX]), ALU.is_ge))
                else:
                    step.done(v.tensor_reduce(lack[:, :], empty_cols[:, :, :], AX, ALU.add))

            def place(h, last=False):
                if last:
                    gates(0)
                v.wait_ge(rank_done, h + 1)
                step.done(v.tensor_tensor(rank[:, :, :], ps_rank.rearrange("p (j e) -> p j e", j=GB),
                                          next_free[0:S, :].unsqueeze(1).to_broadcast([S, GB, E]), ALU.add))
                ranked = step.count
                if last:
                    gates(1)
                step.then(ranked)
                step.done(v.tensor_tensor(rank[:, :, :], rank[:, :, :], choice[:, :, :], ALU.mult))
                v.tensor_tensor(next_free[:, :], next_free[:, :], ps_count, ALU.add).then_inc(rank_kept, 1)
                step.then()
                step.done(v.tensor_reduce(pos[:, :], rank[:, :, :], AX, ALU.add))
                if last:
                    gates(2)
                step.then()
                step.done(v.tensor_copy(pos_i[:, :], pos[:, :]))
                if last:
                    gates(3)
                step.then()
                step.done(v.tensor_single_scalar(place_i[:, 0, :], pos_i[:, :], P - 1, ALU.bitwise_and))
                step.done(v.tensor_single_scalar(place_i[:, 1, :], pos_i[:, :], P.bit_length() - 1, ALU.logical_shift_right))
                if last:
                    gates(4)
                step.then()
                v.tensor_copy(place_f[:, :, :], place_i[:, :, :]).then_inc(place_ready, 1)
                if last:
                    step.then()
                    gates(5)
                v.wait_ge(rank_kept, h + 1)
                v.wait_ge(place_ready, h + 1)
                if last:
                    v.wait_ge(map_done, h)
                own_numbers = group(number, h)
                for j in range(GB):
                    if last and j == 0:
                        empty_columns(0)
                        emptied = step.count
                    if last and j == 1:
                        step.then(emptied)
                        empty_columns(1)
                    step.done(v.tensor_scalar(slot_hot[:, j, :], slot_no[:, :], place_f[:, 0, j:j + 1], None,
                                              ALU.is_equal))
                for j in range(GB):
                    hot = v.tensor_scalar(col_hot[:, j, :], col_no[:, :], place_f[:, 1, j:j + 1], own_numbers[:, j:j + 1],
                                          ALU.is_equal, ALU.mult)
                hot.then_inc(hot_ready, 1)

            def keep_map(h):
                v.wait_ge(map_done, h + 1)
                step.done(v.tensor_tensor(map_T[:, :], map_T[:, :], ps_map, ALU.add))

            FRONT_STEPS, BACK_STEPS = 34, 15

            def take_u(h):
                v.wait_ge(w_done, h + 1)
                v.tensor_scalar(w4[:, :], ps_w, bk_s2[:, 0:1], None, ALU.add).then_inc(w4_ready, 1)
                v.wait_ge(u_done, h + 1)
                v.wait_ge(s_bk_ready, 2 * (h + 1))
                v.tensor_tensor(u_sb[:, :, :], bank_u[:, :].rearrange("p (j d) -> p j d", j=GB), s_bk[:, :, :],
                                ALU.add).then_inc(u_kept, 1)

            def group_front(h, behind, ahead):
                v.wait_ge(m_done, h + 1)
                step.done(v.tensor_tensor(m_sb[:, :, :], bank_m[:, :].rearrange("p (j d) -> p j d", j=GB),
                                          head_mask[:, :].unsqueeze(1).to_broadcast([P, GB, D]), ALU.mult))
                v.wait_ge(w_bv_ready, h + 1)
                step.then()
                v.tensor_tensor(m_sb[:, :, :], m_sb[:, :, :], w_bv[:, :, :], ALU.add).then_inc(m_kept, 1)
                v.wait_ge(mask_folded, h + 1)
                v.tensor_reduce(group(masked, h), mask_fold[:, :, :], AX, ALU.max).then_inc(mask_reduced, 1)
                if behind:
                    choose(h - 1)
                    if ahead:
                        place(h - 1)
                v.wait_ge(o_done, h + 1)
                v.wait_ge(q_bo_ready, h + 1)
                v.tensor_tensor(res[:, :, :], bank_u[0:S, :].rearrange("p (j d) -> p j d", j=GB), q_bo[:, :, :],
                                ALU.add).then_inc(res_ready, 1)
                v.wait_ge(res_ready, h + 1)

                def centred():
                    for j in range(GB):
                        step.done(v.scalar_tensor_tensor(out=res[:, j, :], in0=res[:, j, :], scalar=mv[:, j, 0:1],
                                                         in1=g_rows[:, :], op0=ALU.subtract, op1=ALU.mult))

                layer_norm_stats(res, r_rstd[:, :], h, 0, lambda: step.done(v.memset(unused[:, :], 0.0)), centred)
                v.wait_ge(x_b_ready, h + 1)
                own_rows = group(rows, h)
                for j in range(GB):
                    last = v.scalar_tensor_tensor(out=own_rows[:, j, 0:D], in0=res[:, j, :], scalar=r_rstd[:, j:j + 1],
                                                  in1=x_b[:, j, :], op0=ALU.mult, op1=ALU.add)
                last.then_inc(x1_ready, 1)
                v.wait_ge(x1_ready, h + 1)
                step.done(v.memset(unused[:, :], 0.0))

                def others():
                    if ahead:
                        take_u(h + 1)
                    else:
                        v.memset(unused[:, :], 0.0)

                layer_norm_stats(own_rows, own_rows[:, :, RSTD], h, 1, others,
                                 (lambda: keep_map(h - 1)) if behind and ahead else None)
                v.scalar_tensor_tensor(out=h_nb[:, :], in0=mv[:, 0:GB, 0], scalar=-1.0, in1=own_rows[:, :, RSTD],
                                       op0=ALU.mult, op1=ALU.mult).then_inc(h_nb_ready, 1)
                for j in range(GB // 2):
                    left = v.tensor_scalar(h_sb[:, j, :], own_rows[:, j, 0:D], mv[:, j, 0:1],
                                           own_rows[:, j, RSTD:RSTD + 1], ALU.subtract, ALU.mult)
                left.then_inc(h_left_ready, 1)
                step.done(v.tensor_copy(own_rows[:, :, MEAN], mv[:, 0:GB, 0]))
                if not ahead:
                    place(h - 1)

            take_u(0)
            for h in range(2):
                step.begin(setup_steps + FRONT_STEPS * h)
                group_front(h, behind=h > 0, ahead=True)
                assert step.count == FRONT_STEPS + BACK_STEPS * h, step.count
            with v.Fori(2, NG - 1) as h:
                step.begin(setup_steps + FRONT_STEPS * h + BACK_STEPS * (h - 1))
                group_front(h, behind=True, ahead=True)
            step.begin(setup_steps + FRONT_STEPS * (NG - 1) + BACK_STEPS * (NG - 2))
            group_front(NG - 1, behind=True, ahead=False)
            step.begin(setup_steps + FRONT_STEPS * NG + BACK_STEPS * (NG - 1) - 1)
            choose(NG - 1)
            place(NG - 1, last=True)

            step.then()
            step.done(v.tensor_tensor(lack_before[:, :], lack[0:COLS, :], minus_before[:, :], ALU.mult))
            step.done(v.tensor_tensor(lack_fe[:, :, :], lack[:, :].unsqueeze(1).to_broadcast([P, E, E]), upto[:, :, :],
                                      ALU.mult))
            step.then()
            step.done(v.tensor_reduce(shift[:, :], lack_before[:, :], AX, ALU.add))
            step.done(v.tensor_reduce(lack_upto[:, :], lack_fe[:, :, :], AX, ALU.add))
            v.wait_ge(map_done, NG)
            v.tensor_tensor(map_T[:, :], map_T[:, :], ps_last_map, ALU.add).then_inc(map_kept, 1)
            step.then()
            v.tensor_scalar(picks[:, :], before_tile[:, :], shift[:, :], None, ALU.is_equal).then_inc(picks_ready, 1)
            step.done(v.tensor_tensor(past[:, :, :], lack_upto[:, 0:E - 1].unsqueeze(1).to_broadcast([P, PT, E - 1]),
                                      bound[:, :, :], ALU.is_ge))
            v.wait_ge(token_done, 1)
            step.done(v.tensor_scalar(skip[:, :], ps_token, 0.5, float(SKIP), ALU.is_lt, ALU.mult))
            step.then()
            v.scalar_tensor_tensor(out=token[:, :], in0=ps_token, scalar=-1.0, in1=skip[:, :],
                                   op0=ALU.add, op1=ALU.add).then_inc(token_ready, 1)
            step.done(v.tensor_tensor(past[:, :, :], past[:, :, :], digit[:, :, :, :].rearrange("p w n e -> p (w n) e"),
                                      ALU.mult))
            step.then()
            step.done(v.tensor_reduce(experts_f[:, :], past[:, :, :].rearrange("p (w n) e -> p w (n e)", w=WORDS), AX,
                                      ALU.add))
            step.then()
            v.tensor_scalar(experts_i[:, WORDS:WORDS + 1], lack_upto[:, E - 1:E], COLS - MAIN - 0.5, None, ALU.is_ge)
            v.tensor_copy(experts_i[:, 0:WORDS], experts_f[:, :]).then_inc(table_ready, 1)

            def at(t, column, n):
                return slots[:, bass.ds(t * ROW + column, n)]

            def normalise(t, slot, i):
                v.wait_ge(gathered[t % FLIGHT], 16 * (t // FLIGHT + 1))
                if not (isinstance(t, int) and t < 2):
                    v.wait_ge(h2T_done, t - 1)
                v.tensor_scalar(h2[:, slot, :], at(t, 0, D), at(t, MEAN, 1), at(t, RSTD, 1),
                                ALU.subtract, ALU.mult).then_inc(h2_ready, 1)

            def keep_h2T(t, slot):
                v.wait_ge(h2T_high_kept, t + 1)
                v.tensor_tensor(h2T_low[:, slot, :], bank_x[:, 0:P], h2T_high.bitcast(F32)[:, slot, :],
                                ALU.subtract).then_inc(h2T_low_kept, 1)

            def keep_actT(t, slot):
                v.wait_ge(actT_done, t + 1)
                if t >= 2:
                    v.wait_ge(y_done, t - 1)
                v.tensor_copy(actT[:, slot, :], bank_c[:, :]).then_inc(actT_kept, 1)

            def product(t, slot):
                v.wait_ge(silu_done, t + 1)
                v.wait_ge(g_done, t + 1)
                if t >= 2:
                    v.wait_ge(actT_done, t - 1)
                v.tensor_tensor(act[:, slot, :], gate_s[:, slot, :], bank_g[1][:, :], ALU.mult).then_inc(act_ready, 1)

            def finish(t, slot, i):
                v.wait_ge(y_done, t + 1)
                if not (isinstance(t, int) and t < 2):
                    v.wait_ge(out_written[slot], 16 * i)
                v.scalar_tensor_tensor(out=out_sb[:, slot, :], in0=bank_u[:, 0:D], scalar=at(t, GATE, 1), in1=at(t, 0, D),
                                       op0=ALU.mult, op1=ALU.add).then_inc(out_ready, 1)

            def tiles(start, stop):
                for t in range(start, start + 3):
                    normalise(t, t % 2, t // 2)
                    if t == start:
                        keep_h2T(t, t % 2)
                for t in range(start, stop + 2):
                    if t < stop:
                        product(t, t % 2)
                    if t + 1 < stop:
                        keep_h2T(t + 1, (t + 1) % 2)
                    if start < t <= stop:
                        keep_actT(t - 1, (t - 1) % 2)
                    if t >= start + 2:
                        finish(t - 2, t % 2, (t - 2) // 2)
                    if t + 3 < stop:
                        normalise(t + 3, (t + 3) % 2, (t + 3) // 2)

            tiles(0, MAIN)
            with more_tiles(v):
                tiles(MAIN, TILES)

        @block.tensor
        def _(pe):
            wkT, wvT, wqT, woT = w_T[:, 1, :], w_T[:, 2, :], w_T[:, 0, :], w_T[:, 3, :]

            def stay_busy(bank_, n):
                for _ in range(n):
                    pe.matmul(bank_[:, :], idle[:, 0:P], idle[:, :], start=True, stop=True)

            def gram_of(g, j, between=()):
                between = dict(between)
                pe.wait_ge(ctx_in[j], 32 * (g + 1))
                if not is_first(g) and j % 2 == 0:
                    pe.wait_ge(gram_kept, 2 * (g - 1) + j // 2 + 1)
                to = bank_g[j // 2][:, (j % 2) * CW:(j % 2 + 1) * CW]
                for c in range(NCH):
                    last = pe.matmul(to, ctx_sb[:, j, c, 0:D], ctx_sb[:, j, c, :], start=(c == 0), stop=(c == NCH - 1))
                    if c in between:
                        for stage, of in between[c]:
                            stage(of)
                last.then_inc(gram_done, 1)

            def u_of(h):
                pe.wait_ge(gram_kept, 2 * (h + 1))
                if is_first(h):
                    pe.wait_ge(wT_kept, 1)
                else:
                    pe.wait_ge(res_ready, h)
                for j in range(GB):
                    last = pe.matmul(bank_u[:, j * D:(j + 1) * D], gram[:, j, 0:D], wkT, start=True, stop=True)
                last.then_inc(u_done, 1)

            def w_of(h):
                pe.matmul(ps_w, wkT, gram[:, :, D], start=True, stop=True).then_inc(w_done, 1)

            def m_of(h):
                pe.wait_ge(u_kept, h + 1)
                for j in range(GB):
                    last = pe.matmul(bank_m[:, j * D:(j + 1) * D], u_sb[:, j, :], wvT, start=True, stop=True)
                last.then_inc(m_done, 1)

            def c_of(h):
                pe.wait_ge(m_kept, h + 1)
                pe.wait_ge(q_kept, h + 1)
                for j in range(GB):
                    last = pe.matmul(bank_c[:, j * S:(j + 1) * S], m_sb[:, j, :], qT[:, j * S:(j + 1) * S],
                                     start=True, stop=True)
                last.then_inc(c_done, 1)

            def o_of(h):
                pe.wait_ge(c_kept, h + 1)
                for j in range(GB):
                    last = pe.matmul(bank_u[0:S, j * D:(j + 1) * D], ctxT[:, j * S:(j + 1) * S], woT,
                                     start=True, stop=True)
                last.then_inc(o_done, 1)

            def xT_of(g):
                pe.wait_ge(xln_ready, g + 1)
                if is_first(g):
                    pe.wait_ge(wT_kept, 1)
                else:
                    pe.wait_ge(xlnT_kept, g)
                for j in range(GB):
                    last = pe.transpose(bank_x[:, j * S:(j + 1) * S], xln[:, j, :], ident[0:S, 0:S])
                last.then_inc(xlnT_done, 1)

            def q_of(g):
                pe.wait_ge(xlnT_kept, g + 1)
                if not isinstance(g, int) or g > 1:
                    pe.wait_ge(hT_kept, g - 1)
                    pe.wait_ge(below_ready, g - 1)
                pe.matmul(bank_q[:, 0:GB * S], wqT, xlnT[:, :], start=True, stop=True).then_inc(q_done, 1)

            def hT_of(h):
                pe.wait_ge(h_left_ready, h + 1)
                pe.wait_ge(h_right_ready, h + 1)
                pe.wait_ge(q_kept, h + 2 if not isinstance(h, int) or h < NG - 1 else NG)
                for j in range(GB):
                    last = pe.transpose(bank_q[:, j * S:(j + 1) * S], h_sb[:, j, :], ident[0:S, 0:S])
                last.then_inc(hT_done, 1)

            def logits_of(h):
                pe.wait_ge(hT_kept, h + 1)
                if is_first(h):
                    pe.wait_ge(small_in, 16 * 9)
                for j in range(GB):
                    last = pe.matmul(ps_logit[:, j * E:(j + 1) * E], hT[:, j * S:(j + 1) * S], rw[:, :],
                                     start=True, stop=True)
                last.then_inc(logit_done, 1)

            def ranks_of(h):
                pe.wait_ge(choice_ready, h + 1)
                if is_first(h):
                    pe.wait_ge(pool_set, 9)
                pe.matmul(ps_rank, before[:, :], choice[:, :, :].rearrange("q j e -> q (j e)"), start=True, stop=False)
                for j in range(GB - 1):
                    n = GB - 1 - j
                    pe.matmul(ps_rank[:, (j + 1) * E:].rearrange("q (n e) -> q n e", n=n), ones[:, 0:S],
                              choice[:, j:j + 1, :].to_broadcast([S, n, E]), start=False, stop=(n == 1))
                for j in range(GB):
                    last = pe.matmul(ps_count, ones[:, :], choice[:, j, :], start=(j == 0), stop=(j == GB - 1))
                last.then_inc(rank_done, 1)

            def map_of(h, to=None, start=True, stop=True):
                pe.wait_ge(hot_ready, h + 1)
                for j in range(GB):
                    last = pe.matmul(ps_map if to is None else to, col_hot[:, j, :], slot_hot[:, j, :],
                                     start=start and j == 0, stop=stop and j == GB - 1)
                last.then_inc(map_done, 1)

            pe.wait_ge(idle_set, 1)
            stay_busy(bank_q, 12)
            gram_of(0, 0)
            pe.wait_ge(w_in, 64)
            pe.wait_ge(ident_set, 1)
            for n in range(4):
                last = pe.transpose(bank_x[:, n * D:(n + 1) * D], w_raw[:, n, :], ident[:, :])
            last.then_inc(wT_done, 1)
            gram_of(0, 1)
            gram_of(0, 2)
            gram_of(0, 3)

            def round_of(g):
                behind = not isinstance(g, int) or g > 1
                gram_of(g, 0, {1: [(u_of, g - 1), (w_of, g - 1)],
                               6: [] if behind else [(xT_of, 0)],
                               8: [(m_of, g - 1)],
                               11: [(hT_of, g - 2)] if behind else []})
                gram_of(g, 1, {1: [] if behind else [(q_of, 0)],
                               4: [(c_of, g - 1)],
                               5: [(logits_of, g - 2)] if behind else [],
                               8: [(o_of, g - 1)] if not behind else [],
                               11: [(ranks_of, g - 2)] if behind else []})
                gram_of(g, 2, {1: [(o_of, g - 1)] if behind else [],
                               7: [(xT_of, g)],
                               11: [(q_of, g)]})
                gram_of(g, 3, {6: [(map_of, g - 2)] if behind else []})

            round_of(1)
            round_of(2)
            with pe.Fori(3, NG) as g:
                round_of(g)
            for stage, h in ((u_of, NG - 1), (w_of, NG - 1), (m_of, NG - 1), (hT_of, NG - 2), (c_of, NG - 1),
                             (logits_of, NG - 2), (o_of, NG - 1), (ranks_of, NG - 2)):
                stage(h)
            stay_busy(bank_g[1], 36)
            hT_of(NG - 1)
            logits_of(NG - 1)
            map_of(NG - 2, ps_last_map, stop=False)
            ranks_of(NG - 1)
            stay_busy(bank_g[1], 14)
            map_of(NG - 1, ps_last_map, start=False)
            pe.wait_ge(picks_ready, 1)
            pe.wait_ge(map_kept, 1)
            pe.matmul(ps_token, map_T[:, :], picks[:, :], start=True, stop=True).then_inc(token_done, 1)
            stay_busy(bank_g[1], 12)

            def h2T_of(t, slot):
                pe.wait_ge(h2_ready, t + 1)
                if t >= 1:
                    pe.wait_ge(h2T_low_kept, t)
                pe.transpose(bank_x[:, 0:P], h2[:, slot, :], ident[:, :]).then_inc(h2T_done, 1)

            def up(t, slot, part_, expert):
                if t >= 1:
                    pe.wait_ge(*((silu_done, t) if part_ == 0 else (act_ready, t)))
                own = bass.ds(expert * F2 + part_ * FF, FF)
                pe.wait_ge(h2T_high_kept, t + 1)
                pe.matmul(bank_g[part_][:, :], h2T_high[:, slot, :], w1_high[:, own], start=True, stop=False)
                pe.matmul(bank_g[part_][:, :], h2T_high[:, slot, :], w1_low[:, own], start=False, stop=False)
                pe.wait_ge(h2T_low_kept, t + 1)
                pe.matmul(bank_g[part_][:, :], h2T_low[:, slot, :], w1_high[:, own],
                          start=False, stop=True).then_inc((a_done, g_done)[part_], 1)

            def actT_of(t, slot):
                pe.wait_ge(act_ready, t + 1)
                if t >= 1:
                    pe.wait_ge(actT_kept, t)
                for c in range(FC):
                    last = pe.transpose(bank_c[:, c * P:(c + 1) * P], act[:, slot, c * P:(c + 1) * P], ident[:, :])
                last.then_inc(actT_done, 1)

            def down(t, slot, expert):
                pe.wait_ge(actT_kept, t + 1)
                if t >= 1:
                    pe.wait_ge(out_ready, t)
                for c in range(FC):
                    last = pe.matmul(bank_u[:, 0:D], actT[:, slot, c * P:(c + 1) * P],
                                     w2_sb[:, bass.ds(expert * (FC * D) + c * D, D)], start=(c == 0), stop=(c == FC - 1))
                last.then_inc(y_done, 1)

            pe.wait_ge(table_ready, 1)
            words = [pe.value_load(experts_i[0:1, w:w + 1], min_val=0, max_val=8 ** PACK - 1) for w in range(WORDS)]
            experts = [(words[t // PACK] >> (3 * (t % PACK))) & 7 for t in range(TILES)]
            pe.wait_ge(low_kept, NG)
            pe.wait_ge(w2_in, 16 * NG)
            stay_busy(bank_g[1], 4)

            def tiles(start, stop):
                h2T_of(start, start % 2)
                for t in range(start, stop + 2):
                    if t < stop:
                        up(t, t % 2, 0, experts[t])
                    if t + 1 < stop:
                        h2T_of(t + 1, (t + 1) % 2)
                    if t < stop:
                        up(t, t % 2, 1, experts[t])
                    if start < t <= stop:
                        actT_of(t - 1, (t - 1) % 2)
                    if t >= start + 2:
                        down(t - 2, t % 2, experts[t - 2])

            tiles(0, MAIN)
            with more_tiles(pe):
                tiles(MAIN, TILES)


def kernel(**inputs):
    import concourse.bacc as bacc
    import numpy as np
    from concourse.bass_utils import run_bass_kernel_spmd

    names = ("x", "ctx_1024", "mask_Bx1xSxS2_bf0", "L0_xattn_wq_w", "L0_xattn_wq_b", "L0_xattn_wk_w", "L0_xattn_wk_b",
             "L0_xattn_wv_w", "L0_xattn_wv_b", "L0_xattn_wo_w", "L0_xattn_wo_b", "L0_xattn_ln_g", "L0_xattn_ln_b",
             "L0_ffn_router_w", "L0_ffn_router_b", "L0_ffn_w1", "L0_ffn_w2")
    nc = bacc.Bacc("TRN2", target_bir_lowering=False, num_devices=1)
    arrays, args = {}, []
    for name in names:
        a = np.ascontiguousarray(inputs[name])
        arrays[name] = a
        args.append(nc.dram_tensor(name, a.shape, mybir.dt.from_np(a.dtype), kind="ExternalInput").ap())
    out = nc.dram_tensor("out", arrays["x"].shape, F32, kind="ExternalOutput").ap()
    build(nc, *args, out)
    return run_bass_kernel_spmd(nc, [arrays], core_ids=[0]).results[0]["out"]
```
